# Optimizing a Trainium2 kernel written in Bass

```python
import numpy as np
import jax
import jax.numpy as jnp

def _softmax(x, axis=-1):
    return jax.nn.softmax(x, axis=axis)

def _gelu(x):
    return jax.nn.gelu(x, approximate=True)

def _silu(x):
    return jax.nn.silu(x)

def _sigmoid(x):
    return jax.nn.sigmoid(x)

def _layernorm(x, axis=-1, eps=1e-05):
    m = jnp.mean(x, axis=axis, keepdims=True)
    v = jnp.var(x, axis=axis, keepdims=True)
    return (x - m) / jnp.sqrt(v + eps)

def _scatter_add(tgt, idx, src, axis=0):
    return tgt.at[idx].add(src)

def _segment_sum(src, seg, n):
    return jax.ops.segment_sum(src, seg, n)
kernel_name = 'mk_adaln_d2_jaxref_r8_40842a'

def setup_inputs(seed: int=0):
    np.random.seed(seed)
    _w = jnp.asarray

    def _L0_attn_setup():
        import jax, jax.numpy as jnp
        import numpy as np
        B, L, D, N = (4, 256, 128, 16)

        def _layernorm(x, g, b, eps=1e-05):
            mu = jnp.mean(x, axis=-1, keepdims=True)
            var = jnp.mean(jnp.square(x - mu), axis=-1, keepdims=True)
            return (x - mu) * jax.lax.rsqrt(var + eps) * g + b

        def _silu(x):
            return x * jax.nn.sigmoid(x)

        def _depthwise_conv(x, w):
            xc = x.transpose(0, 2, 1)
            y = jax.lax.conv_general_dilated(xc, w, window_strides=(1,), padding=[(1, 1)], feature_group_count=xc.shape[1], dimension_numbers=('NCH', 'OIH', 'NCH'))
            return y.transpose(0, 2, 1)

        def _selective_scan(u, A_log, D_skip, W_dt, b_dt, W_B, W_C):
            A = -jnp.exp(A_log)
            dt = jax.nn.softplus(u @ W_dt + b_dt)
            Bt = u @ W_B
            Ct = u @ W_C

            def step(h, inp):
                dt_t, B_t, C_t, u_t = inp
                dA = jnp.exp(dt_t[..., None] * A)
                h = dA * h + (dt_t * u_t)[..., None] * B_t[:, None, :]
                y = jnp.einsum('bdn,bn->bd', h, C_t)
                return (h, y)
            h0 = jnp.zeros((u.shape[0], u.shape[2], A.shape[1]), u.dtype)
            xs = (dt.transpose(1, 0, 2), Bt.transpose(1, 0, 2), Ct.transpose(1, 0, 2), u.transpose(1, 0, 2))
            _, ys = jax.lax.scan(step, h0, xs)
            return ys.transpose(1, 0, 2) + u * D_skip
        key = jax.random.key(seed)
        ks = jax.random.split(key, 12)
        s = 1.0 / np.sqrt(D)
        inp = {'x': jax.random.normal(ks[0], (B, L, D), jnp.float32), 'ln_g': jnp.ones((D,), jnp.float32), 'ln_b': jnp.zeros((D,), jnp.float32), 'w1_w': jax.random.normal(ks[1], (D, D), jnp.float32) * s, 'w1_b': jnp.zeros((D,), jnp.float32), 'v1_w': jax.random.normal(ks[2], (D, D), jnp.float32) * s, 'v1_b': jnp.zeros((D,), jnp.float32), 'w2_w': jax.random.normal(ks[3], (D, D), jnp.float32) * s, 'w2_b': jnp.zeros((D,), jnp.float32), 'conv_w': jax.random.normal(ks[4], (D, 1, 3), jnp.float32) * (1.0 / np.sqrt(3.0)), 'A_log': jnp.log(jnp.broadcast_to(jnp.arange(1, N + 1, dtype=jnp.float32), (D, N))), 'D_skip': jnp.ones((D,), jnp.float32), 'W_dt': jax.random.normal(ks[5], (D, D), jnp.float32) * (s * 0.1), 'b_dt': jnp.full((D,), -4.0, jnp.float32), 'W_B': jax.random.normal(ks[6], (D, N), jnp.float32) * s, 'W_C': jax.random.normal(ks[7], (D, N), jnp.float32) * s}
        return inp
    _L0_attn_in = _L0_attn_setup()

    def _L0_ffn_setup():
        import jax, jax.numpy as jnp
        import numpy as np
        import math
        E = 8
        K = 2
        CF = 1.2
        D = 128
        H = 512
        key = jax.random.key(seed)
        k0, k1, k2, k3 = jax.random.split(key, 4)
        B, T = (8, 256)
        x_btd = jax.random.normal(k0, (B, T, D), jnp.float32)
        Wr = jax.random.normal(k1, (D, E), jnp.float32) / np.sqrt(D)
        br = jnp.zeros((E,), jnp.float32)
        W1 = jax.random.normal(k2, (E, D, H), jnp.float32) / np.sqrt(D)
        b1 = jnp.zeros((E, H), jnp.float32)
        W2 = jax.random.normal(k3, (E, H, D), jnp.float32) / np.sqrt(H)
        b2 = jnp.zeros((E, D), jnp.float32)
        return dict(x_btd=x_btd, Wr=Wr, br=br, W1=W1, b1=b1, W2=W2, b2=b2)
    _L0_ffn_in = _L0_ffn_setup()
    _L0_c = _w((lambda *s: np.random.randn(*s).astype(np.float32) * 0.05)(1, 128))
    _L0_wmod = _w((lambda *s: np.random.randn(*s).astype(np.float32) * 0.05)(128, 6 * 128) * 128 ** (-0.5))

    def _L1_attn_setup():
        import jax, jax.numpy as jnp
        import numpy as np
        B, L, E, H = (2, 256, 128, 16)
        HD = E // H
        THETA = 10000.0

        def _rope_tables(seq_len, dim, dtype):
            inv_freq = 1.0 / THETA ** (jnp.arange(0, dim, 2, dtype=jnp.float32) / dim)
            freqs = jnp.arange(seq_len, dtype=jnp.float32)[:, None] * inv_freq[None, :]
            freqs = jnp.repeat(freqs, 2, axis=-1)
            return (jnp.cos(freqs).astype(dtype), jnp.sin(freqs).astype(dtype))

        def _rotate_half(x):
            x2 = x.reshape(*x.shape[:-1], -1, 2)
            x2 = jnp.stack([-x2[..., 1], x2[..., 0]], axis=-1)
            return x2.reshape(x.shape)

        def _apply_rope(x, cos, sin):
            return x * cos[None, None] + _rotate_half(x) * sin[None, None]
        key = jax.random.key(seed)
        ks = jax.random.split(key, 9)
        s = 1.0 / np.sqrt(E)
        return {'x': jax.random.normal(ks[0], (B, L, E), jnp.float32), 'Wq': jax.random.normal(ks[1], (E, E), jnp.float32) * s, 'bq': jax.random.normal(ks[2], (E,), jnp.float32) * 0.01, 'Wk': jax.random.normal(ks[3], (E, E), jnp.float32) * s, 'bk': jax.random.normal(ks[4], (E,), jnp.float32) * 0.01, 'Wv': jax.random.normal(ks[5], (E, E), jnp.float32) * s, 'bv': jax.random.normal(ks[6], (E,), jnp.float32) * 0.01, 'Wo': jax.random.normal(ks[7], (E, E), jnp.float32) * s, 'bo': jax.random.normal(ks[8], (E,), jnp.float32) * 0.01}
    _L1_attn_in = _L1_attn_setup()

    def _L1_ffn_setup():
        import jax, jax.numpy as jnp
        import numpy as np
        N_EXPERTS = 8
        TOP_K = 2
        key = jax.random.key(seed)
        k1, k2, k3, k4 = jax.random.split(key, 4)
        B, T, C, H, E = (2, 256, 128, 512, N_EXPERTS)
        x = jax.random.normal(k1, (B, T, C), dtype=jnp.float32)
        router_w = jax.random.normal(k2, (E, C), dtype=jnp.float32) * 0.02
        w1 = jax.random.normal(k3, (E, C, H), dtype=jnp.float32) * (1.0 / np.sqrt(C))
        w2 = jax.random.normal(k4, (E, H, C), dtype=jnp.float32) * (1.0 / np.sqrt(H))
        return {'x': x, 'router_w': router_w, 'w1': w1, 'w2': w2}
    _L1_ffn_in = _L1_ffn_setup()
    _L1_c = _w((lambda *s: np.random.randn(*s).astype(np.float32) * 0.05)(1, 128))
    _L1_wmod = _w((lambda *s: np.random.randn(*s).astype(np.float32) * 0.05)(128, 6 * 128) * 128 ** (-0.5))
    _d = {'L0_attn_x': _L0_attn_in['x'], 'L0_attn_ln_g': _L0_attn_in['ln_g'], 'L0_attn_ln_b': _L0_attn_in['ln_b'], 'L0_attn_w1_w': _L0_attn_in['w1_w'], 'L0_attn_w1_b': _L0_attn_in['w1_b'], 'L0_attn_v1_w': _L0_attn_in['v1_w'], 'L0_attn_v1_b': _L0_attn_in['v1_b'], 'L0_attn_w2_w': _L0_attn_in['w2_w'], 'L0_attn_w2_b': _L0_attn_in['w2_b'], 'L0_attn_conv_w': _L0_attn_in['conv_w'], 'L0_attn_A_log': _L0_attn_in['A_log'], 'L0_attn_D_skip': _L0_attn_in['D_skip'], 'L0_attn_W_dt': _L0_attn_in['W_dt'], 'L0_attn_b_dt': _L0_attn_in['b_dt'], 'L0_attn_W_B': _L0_attn_in['W_B'], 'L0_attn_W_C': _L0_attn_in['W_C'], 'L0_ffn_Wr': _L0_ffn_in['Wr'], 'L0_ffn_br': _L0_ffn_in['br'], 'L0_ffn_W1': _L0_ffn_in['W1'], 'L0_ffn_b1': _L0_ffn_in['b1'], 'L0_ffn_W2': _L0_ffn_in['W2'], 'L0_ffn_b2': _L0_ffn_in['b2'], 'L0_c': _L0_c, 'L0_wmod': _L0_wmod, 'L1_attn_Wq': _L1_attn_in['Wq'], 'L1_attn_bq': _L1_attn_in['bq'], 'L1_attn_Wk': _L1_attn_in['Wk'], 'L1_attn_bk': _L1_attn_in['bk'], 'L1_attn_Wv': _L1_attn_in['Wv'], 'L1_attn_bv': _L1_attn_in['bv'], 'L1_attn_Wo': _L1_attn_in['Wo'], 'L1_attn_bo': _L1_attn_in['bo'], 'L1_ffn_router_w': _L1_ffn_in['router_w'], 'L1_ffn_w1': _L1_ffn_in['w1'], 'L1_ffn_w2': _L1_ffn_in['w2'], 'L1_c': _L1_c, 'L1_wmod': _L1_wmod}
    _x0 = _d['L0_attn_x']
    _d['L0_attn_x'] = jax.random.normal(jax.random.fold_in(jax.random.key(seed), 1), (1, 2048, 128), dtype=_x0.dtype)
    del _x0
    return _d

def reference(L0_attn_x, L0_attn_ln_g, L0_attn_ln_b, L0_attn_w1_w, L0_attn_w1_b, L0_attn_v1_w, L0_attn_v1_b, L0_attn_w2_w, L0_attn_w2_b, L0_attn_conv_w, L0_attn_A_log, L0_attn_D_skip, L0_attn_W_dt, L0_attn_b_dt, L0_attn_W_B, L0_attn_W_C, L0_ffn_Wr, L0_ffn_br, L0_ffn_W1, L0_ffn_b1, L0_ffn_W2, L0_ffn_b2, L0_c, L0_wmod, L1_attn_Wq, L1_attn_bq, L1_attn_Wk, L1_attn_bk, L1_attn_Wv, L1_attn_bv, L1_attn_Wo, L1_attn_bo, L1_ffn_router_w, L1_ffn_w1, L1_ffn_w2, L1_c, L1_wmod):

    def _L0_attn_ref(x, ln_g, ln_b, w1_w, w1_b, v1_w, v1_b, w2_w, w2_b, conv_w, A_log, D_skip, W_dt, b_dt, W_B, W_C):
        import jax, jax.numpy as jnp
        import numpy as np
        B, L, D, N = (4, 256, 128, 16)

        def _layernorm(x, g, b, eps=1e-05):
            mu = jnp.mean(x, axis=-1, keepdims=True)
            var = jnp.mean(jnp.square(x - mu), axis=-1, keepdims=True)
            return (x - mu) * jax.lax.rsqrt(var + eps) * g + b

        def _silu(x):
            return x * jax.nn.sigmoid(x)

        def _depthwise_conv(x, w):
            xc = x.transpose(0, 2, 1)
            y = jax.lax.conv_general_dilated(xc, w, window_strides=(1,), padding=[(1, 1)], feature_group_count=xc.shape[1], dimension_numbers=('NCH', 'OIH', 'NCH'))
            return y.transpose(0, 2, 1)

        def _selective_scan(u, A_log, D_skip, W_dt, b_dt, W_B, W_C):
            A = -jnp.exp(A_log)
            dt = jax.nn.softplus(u @ W_dt + b_dt)
            Bt = u @ W_B
            Ct = u @ W_C

            def step(h, inp):
                dt_t, B_t, C_t, u_t = inp
                dA = jnp.exp(dt_t[..., None] * A)
                h = dA * h + (dt_t * u_t)[..., None] * B_t[:, None, :]
                y = jnp.einsum('bdn,bn->bd', h, C_t)
                return (h, y)
            h0 = jnp.zeros((u.shape[0], u.shape[2], A.shape[1]), u.dtype)
            xs = (dt.transpose(1, 0, 2), Bt.transpose(1, 0, 2), Ct.transpose(1, 0, 2), u.transpose(1, 0, 2))
            _, ys = jax.lax.scan(step, h0, xs)
            return ys.transpose(1, 0, 2) + u * D_skip
        x_norm = _layernorm(x, ln_g, ln_b)
        x1 = x_norm @ w1_w + w1_b
        x_conv = _silu(_depthwise_conv(x1, conv_w))
        x_ssm = _selective_scan(x_conv, A_log, D_skip, W_dt, b_dt, W_B, W_C)
        v = _silu(x_norm @ v1_w + v1_b)
        return x_ssm * v @ w2_w + w2_b

    def _L0_ffn_ref(x_btd, Wr, br, W1, b1, W2, b2):
        import jax, jax.numpy as jnp
        import numpy as np
        import math
        E = 8
        K = 2
        CF = 1.2
        D = 128
        H = 512
        B, T, Dm = x_btd.shape
        N = B * T
        x = x_btd.reshape(N, Dm)
        cap = int(math.ceil(CF * N / E))
        probs = jax.nn.softmax(x @ Wr + br, axis=-1)
        gates, ids = jax.lax.top_k(probs, K)
        flat_ids = ids.reshape(-1)
        flat_g = gates.reshape(-1)
        M = N * K
        order = jnp.lexsort((-flat_g, flat_ids))
        s_ids = flat_ids[order]
        s_tok = (order // K).astype(jnp.int32)
        s_g = flat_g[order]
        counts = jnp.bincount(flat_ids, length=E)
        starts = jnp.concatenate([jnp.zeros((1,), counts.dtype), jnp.cumsum(counts)[:-1]])
        rank = jnp.arange(M) - starts[s_ids]
        valid = rank < cap
        pos = jnp.where(valid, s_ids * cap + rank, E * cap)
        disp_tok = jnp.zeros((E * cap + 1,), jnp.int32).at[pos].set(s_tok)[:E * cap]
        disp_g = jnp.zeros((E * cap + 1,), x.dtype).at[pos].set(s_g)[:E * cap]
        xg = x[disp_tok].reshape(E, cap, Dm)
        h = jax.nn.silu(jnp.einsum('ecd,edh->ech', xg, W1) + b1[:, None, :])
        out = jnp.einsum('ech,ehd->ecd', h, W2) + b2[:, None, :]
        gated = out * disp_g.reshape(E, cap, 1)
        y = jnp.zeros((N, Dm), x.dtype).at[disp_tok].add(gated.reshape(E * cap, Dm))
        return y.reshape(B, T, Dm)

    def _L1_attn_ref(x, Wq, bq, Wk, bk, Wv, bv, Wo, bo):
        import jax, jax.numpy as jnp
        import numpy as np
        B, L, E, H = (2, 256, 128, 16)
        HD = E // H
        THETA = 10000.0

        def _rope_tables(seq_len, dim, dtype):
            inv_freq = 1.0 / THETA ** (jnp.arange(0, dim, 2, dtype=jnp.float32) / dim)
            freqs = jnp.arange(seq_len, dtype=jnp.float32)[:, None] * inv_freq[None, :]
            freqs = jnp.repeat(freqs, 2, axis=-1)
            return (jnp.cos(freqs).astype(dtype), jnp.sin(freqs).astype(dtype))

        def _rotate_half(x):
            x2 = x.reshape(*x.shape[:-1], -1, 2)
            x2 = jnp.stack([-x2[..., 1], x2[..., 0]], axis=-1)
            return x2.reshape(x.shape)

        def _apply_rope(x, cos, sin):
            return x * cos[None, None] + _rotate_half(x) * sin[None, None]
        b, l, e = x.shape
        q = (x @ Wq.T + bq).reshape(b, l, H, HD).transpose(0, 2, 1, 3)
        k = (x @ Wk.T + bk).reshape(b, l, H, HD).transpose(0, 2, 1, 3)
        v = (x @ Wv.T + bv).reshape(b, l, H, HD).transpose(0, 2, 1, 3)
        cos, sin = _rope_tables(l, HD, x.dtype)
        q = _apply_rope(q, cos, sin)
        k = _apply_rope(k, cos, sin)
        scale = 1.0 / np.sqrt(HD)
        scores = jnp.einsum('bhsd,bhed->bhse', q, k) * scale
        attn = jax.nn.softmax(scores, axis=-1)
        out = jnp.einsum('bhse,bhed->bhsd', attn, v)
        out = out.transpose(0, 2, 1, 3).reshape(b, l, e)
        return out @ Wo.T + bo

    def _L1_ffn_ref(x, router_w, w1, w2):
        import jax, jax.numpy as jnp
        import numpy as np
        N_EXPERTS = 8
        TOP_K = 2
        B, T, C = x.shape
        E = N_EXPERTS
        xf = x.reshape(-1, C)
        logits = jnp.einsum('nc,ec->ne', xf, router_w)
        probs = jax.nn.softmax(logits, axis=-1)
        top_w, top_i = jax.lax.top_k(probs, TOP_K)
        top_w = top_w / jnp.sum(top_w, axis=-1, keepdims=True)
        comb = jnp.einsum('nk,nke->ne', top_w, jax.nn.one_hot(top_i, E, dtype=xf.dtype))
        h = jax.nn.gelu(jnp.einsum('nc,ech->enh', xf, w1), approximate=False)
        y = jnp.einsum('enh,ehc->enc', h, w2)
        out = jnp.einsum('ne,enc->nc', comb, y)
        return out.reshape(B, T, C)
    x = L0_attn_x
    mod = (_silu(L0_c) @ L0_wmod).reshape(L0_c.shape[0], 6, 1, -1)
    sa, ca, ga, sb, cb, gb = (mod[:, 0], mod[:, 1], mod[:, 2], mod[:, 3], mod[:, 4], mod[:, 5])
    ga = (2 * (ga >= 0) - 1) * jnp.maximum(jnp.abs(ga), 0.25)
    gb = (2 * (gb >= 0) - 1) * jnp.maximum(jnp.abs(gb), 0.25)
    h = _layernorm(x, axis=-1) * (1 + ca) + sa
    x = x + ga * _L0_attn_ref(h, L0_attn_ln_g, L0_attn_ln_b, L0_attn_w1_w, L0_attn_w1_b, L0_attn_v1_w, L0_attn_v1_b, L0_attn_w2_w, L0_attn_w2_b, L0_attn_conv_w, L0_attn_A_log, L0_attn_D_skip, L0_attn_W_dt, L0_attn_b_dt, L0_attn_W_B, L0_attn_W_C)
    h = _layernorm(x, axis=-1) * (1 + cb) + sb
    x = x + gb * _L0_ffn_ref(h, L0_ffn_Wr, L0_ffn_br, L0_ffn_W1, L0_ffn_b1, L0_ffn_W2, L0_ffn_b2)
    mod = (_silu(L1_c) @ L1_wmod).reshape(L1_c.shape[0], 6, 1, -1)
    sa, ca, ga, sb, cb, gb = (mod[:, 0], mod[:, 1], mod[:, 2], mod[:, 3], mod[:, 4], mod[:, 5])
    ga = (2 * (ga >= 0) - 1) * jnp.maximum(jnp.abs(ga), 0.25)
    gb = (2 * (gb >= 0) - 1) * jnp.maximum(jnp.abs(gb), 0.25)
    h = _layernorm(x, axis=-1) * (1 + ca) + sa
    x = x + ga * _L1_attn_ref(h, L1_attn_Wq, L1_attn_bq, L1_attn_Wk, L1_attn_bk, L1_attn_Wv, L1_attn_bv, L1_attn_Wo, L1_attn_bo)
    h = _layernorm(x, axis=-1) * (1 + cb) + sb
    x = x + gb * _L1_ffn_ref(h, L1_ffn_router_w, L1_ffn_w1, L1_ffn_w2)
    return x

_drawn_inputs = setup_inputs


def setup_inputs(seed=0):
    import zlib

    import numpy as np

    out = dict(_drawn_inputs(seed))
    spreads = {'L0_attn_ln_g': (1.0, 0.2),
     'L0_attn_ln_b': (0.0, 0.426),
     'L0_attn_w1_b': (0.0, 0.415),
     'L0_attn_v1_b': (0.0, 0.486),
     'L0_attn_w2_b': (0.0, 0.271),
     'L0_attn_D_skip': (1.0, 0.2),
     'L0_attn_b_dt': (-4.0, 0.6),
     'L0_ffn_br': (0.0, 0.492),
     'L0_ffn_b1': (0.0, 0.8),
     'L0_ffn_b2': (0.0, 0.558)}
    factors = {'L0_attn_A_log': 4.257,
     'L0_attn_W_dt': 8.0,
     'L0_attn_W_B': 3.225,
     'L0_attn_W_C': 3.062,
     'L1_attn_Wq': 3.292,
     'L1_attn_bq': 8.0,
     'L1_attn_Wk': 3.173,
     'L1_attn_bk': 8.0,
     'L1_attn_Wv': 2.873,
     'L1_attn_bv': 8.0,
     'L1_attn_Wo': 2.787,
     'L1_attn_bo': 38.598}
    for name, (base, spread) in spreads.items():
        noise = np.random.default_rng([zlib.crc32(name.encode()), seed]).standard_normal(out[name].shape)
        drawn = base * np.exp(spread * noise) if base else spread * noise
        out[name] = jnp.asarray(drawn.astype(out[name].dtype))
    for name, factor in factors.items():
        out[name] = (out[name] * factor).astype(out[name].dtype)
    return out
```

```python
from contextlib import ExitStack

import numpy as np

import concourse.bass as bass
from concourse import mybir

F32 = mybir.dt.float32
BF16 = mybir.dt.bfloat16
ALU = mybir.AluOpType
ACT = mybir.ActivationFunctionType
AX = mybir.AxisListType

D = 128
L = 2048
C = 512
NC = L // C
TILES = L // 128
TPC = C // 128
HALF = L // 2
NS = 16
EPS = 1e-5

COLS = ["ln_g", "ln_b", "w1_b", "v1_b", "w2_b", "b_dt", "D_skip", "conv0", "conv1", "conv2",
        "c0", "c1", "bq", "bk", "bo", "part1", "part2"]
COL = {n: i for i, n in enumerate(COLS)}
A_LOG = len(COLS)
NCOLS = A_LOG + NS
MATS = ["w1", "v1", "w2", "W_dt", "W_BC", "WqT", "WkT", "WvT", "WoT", "ident", "mean", "group", "rotate", "bv_rows"]
MAT = {n: i for i, n in enumerate(MATS)}
SA, CA, GA, SB, CB, GB = range(6)

NE = 8
HC = 4
CAP = 308
REP = 128 // NE
ROUNDS = 8
I32 = mybir.dt.int32


NH = 16
HD = D // NH
UN = 4
KT = TILES
SCALE = float(HD) ** -0.5
THETA = 10000.0
SHIFT = 2
GROUP = 3 * HD
VM = 32
SPAN = L // HD
STORES = NC + 1
STACK_LOADS = 13


def maxima_stream():
    found = []
    for step in range(KT):
        found += [(step, "scores", (step, c)) for c in range(NC)]
        if step and step % 4 == 0:
            found.append((step, "row", step // 4 - 1))
    found.append((KT, "row", KT // 4 - 1))
    return found


STREAM = maxima_stream()
SN = len(STREAM)
RING = 3
assert SN % RING == 2
SCORES = KT * NC
ROWS = KT // 4
AHEAD = 2


def build(nc, xT_in, cols_in, mats_in, wmod_in, bcsel_in, router_in, digits_in, cos_in, sin_in, zero_in, spread_in, moe_in, out):
    with ExitStack() as ctx:
        def sb(name, shape, dt=F32):
            return ctx.enter_context(nc.sbuf_tensor(name, shape, dt))

        def phase():
            inner = ExitStack()
            return inner, lambda name, shape, dt=F32: inner.enter_context(nc.sbuf_tensor(name, shape, dt))

        def sem(name):
            return ctx.enter_context(nc.semaphore(name))

        psum = ctx.enter_context(nc.psum_tensor("psum", [128, 8, C], F32))

        def banks(b, n):
            return psum[:, b:b + n, :].rearrange("p b c -> p (b c)")

        cols = sb("cols", [128, NCOLS])
        mats = sb("mats", [128, len(MATS), 128])
        wmod = sb("wmod", [128, 12, 128])
        bcsel_f = sb("bcsel_f", [128, 2 * NS])
        bcsel = sb("bcsel", [128, 2 * NS], BF16)
        silu_c = sb("silu_c", [128, 2])
        mod = sb("mod", [128, 12])
        gate_sign = sb("gate_sign", [128, 4])
        gate_size = sb("gate_size", [128, 4])
        gated_w2b = sb("gated_w2b", [128, 1])
        diag_skip = sb("diag_skip", [128, 128])
        eps_col = sb("eps_col", [128, 1])

        xT = sb("xT", [128, L])
        h0T = sb("h0T", [128, L])
        normT = sb("normT", [128, L])
        ln_xc = sb("ln_xc", [128, L])
        ln_sq = sb("ln_sq", [128, 2, C])
        ln_std = sb("ln_std", [128, 2, TPC])
        ln_rstd = sb("ln_rstd", [128, 2, TPC])
        ln_xn = sb("ln_xn", [128, 2, C])

        def col(name):
            return cols[:, COL[name]:COL[name] + 1]

        def mat(name):
            return mats[:, MAT[name], :]

        def modc(layer, j):
            return mod[:, 6 * layer + j:6 * layer + j + 1]

        proj_o = sb("proj_o", [128, 2, C])
        router = sb("router", [128, 2 * NE + 2 * NE + ROUNDS])
        router_w = [router[:, 0:NE], router[:, NE:2 * NE]]
        expert_no = router[:, 2 * NE:3 * NE]
        router_b = router[:, 3 * NE:4 * NE]
        digit_size = router[:, 4 * NE:4 * NE + ROUNDS]
        digits = sb("digits", [128, ROUNDS], I32)
        rt = {n: sb(f"rt_{n}", [128, TILES, NE]) for n in ["logit", "prob", "eq", "best1", "rest", "best2", "gate"]}
        rs = {n: sb(f"rs_{n}", [128, TILES]) for n in ["max", "sum", "inv", "top1", "no", "top2"]}
        gate_wide = ln_xc[:].rearrange("p (t e r) -> p t e r", t=TILES, e=NE)
        gates_rep = h0T
        thr = {n: sb(f"thr_{n}", [128, 1], I32) for n in ["low", "try", "add"]}
        thr_f = {n: sb(f"thr_{n}", [128, 1]) for n in ["count", "keep", "quota"]}
        w1s = sb("w1s", [128, 2, HC * 128])
        w2s = sb("w2s", [128, 2, HC, 128])
        b1s = sb("b1s", [128, 2, HC])
        b2s = sb("b2s", [128, 2, 1])
        gates_dram = [nc.dram_tensor(f"gates_dram{n}", (NE, L), F32).ap() for n in range(2)]

        ident_b = sb("ident_b", [128, 128], BF16)
        tile_max = sb("tile_max", [128, KT, NC])
        row_max = sb("row_max", [128, 4, 4])
        max_parts = sb("max_parts", [128, 4, 4, SHIFT], BF16)
        gated_bo = sb("gated_bo", [128, 1])
        o_sb = sb("o_sb", [128, 2, C])
        sums = sb("sums", [128, SPAN])
        spread_sums = sb("spread_sums", [128, HD, 128])

        ssm_scope, ssm_sb = phase()
        x1pad = ssm_sb("x1pad", [128, L + 2])
        conv_a = ssm_sb("conv_a", [128, 2, C])
        conv_b = ssm_sb("conv_b", [128, 2, C])
        vT = ssm_sb("vT", [128, L])
        uT = ssm_sb("uT", [128, L])
        dt_x = ssm_sb("dt_x", [128, L])
        dt_z = ssm_sb("dt_z", [128, L])
        dt_w = ssm_sb("dt_w", [128, L])
        dt_ln = ssm_sb("dt_ln", [128, L])
        conv_y, bc_r1, dt_abs, dt_e, dt_r = h0T, normT, dt_z, dt_z, dt_ln
        dtT = ssm_sb("dtT", [128, L])
        dtuT = ssm_sb("dtuT", [128, L])
        bc_p1 = ssm_sb("bc_p1", [128, L], BF16)
        bc_p2 = ssm_sb("bc_p2", [128, L], BF16)
        bc_parts = ssm_sb("bc_parts", [128, L], BF16)
        expA = ssm_sb("expA", [128, NS])
        negA = ssm_sb("negA", [128, NS])
        ssm_dA = ssm_sb("ssm_dA", [128, 2, HALF])
        ssm_b = dt_z[:].rearrange("p (k t) -> p k t", k=2)
        ssm_dBu = ssm_sb("ssm_dBu", [128, 2, HALF])
        ssm_h = ssm_sb("ssm_h", [128, 2, HALF])
        ssm_g = ssm_sb("ssm_g", [128, 2, HALF])
        ssm_carry = ssm_sb("ssm_carry", [128, NS])
        yvT = dt_x
        ssm_scope.close()

        moe_scope, moe_sb = phase()
        gate_eq = moe_sb("gate_eq", [128, L])
        gate_rank = moe_sb("gate_rank", [128, L])
        gate_valid = moe_sb("gate_valid", [128, L])
        gate_bc = moe_sb("gate_bc", [128, 2, L])
        hidden = moe_sb("hidden", [128, 2, HC, C])
        gated = moe_sb("gated", [128, 2, C])
        moe_acc = moe_sb("moe_acc", [128, L])
        moe_scope.close()

        attn_scope, attn_sb = phase()
        qkT = [attn_sb(n, [128, L]) for n in ("qT", "kT")]
        cosT = attn_sb("cosT", [128, L])
        sinT = attn_sb("sinT", [128, L])
        attn_scope.close()
        attn_scope, attn_sb = phase()
        probs = attn_sb("probs", [128, 4, L])
        qk_parts = [attn_sb(n, [128, 3, L], BF16) for n in ("q_parts", "k_parts")]
        rope_cos = attn_sb("rope_cos", [128, 2, C])
        rope_sin = attn_sb("rope_sin", [128, 2, C])
        qk_rest = attn_sb("qk_rest", [128, 2, C])
        q_stack = attn_sb("q_stack", [128, UN, L], BF16)
        k_stack = attn_sb("k_stack", [128, UN, L], BF16)
        v_all = attn_sb("v_all", [128, KT, NH, HD + 1])
        v_head = attn_sb("v_head", [128, UN, KT, VM])
        attn_scope.close()
        attnT = h0T
        parts_dram = [nc.dram_tensor(n, (128, 3, L), BF16).ap() for n in ("q_dram", "k_dram")]
        o_dram = nc.dram_tensor("o_dram", (128, NC, C), F32).ap()
        sums_dram = nc.dram_tensor("sums_dram", (NH, NC, C), F32).ap()

        params_in = sem("params_in")
        x_in = [sem(f"x_in{c}") for c in range(NC)]
        wmod_loaded = sem("wmod_loaded")
        router_loaded = sem("router_loaded")
        out_done = sem("out_done")
        silu_c_ready = sem("silu_c_ready")
        mod_ps_ready = sem("mod_ps_ready")
        mod_step = sem("mod_step")
        mod_ready = sem("mod_ready")
        misc_step = sem("misc_step")
        bcsel_ready = sem("bcsel_ready")
        diag_ready = sem("diag_ready")
        ln_in_ready = sem("ln_in_ready")
        ln_mean_ready = sem("ln_mean_ready")
        ln_xc_ready = sem("ln_xc_ready")
        ln_sq_ready = sem("ln_sq_ready")
        ln_var_ready = sem("ln_var_ready")
        ln_std_ready = sem("ln_std_ready")
        ln_rstd_ready = sem("ln_rstd_ready")
        ln_xn_ready = sem("ln_xn_ready")
        ln_bc_ready = sem("ln_bc_ready")
        normed_ready = sem("normed_ready")
        x1_ps = sem("x1_ps")
        v_ps = sem("v_ps")
        x1_ready = sem("x1_ready")
        v_ready = sem("v_ready")
        pad_ready = sem("pad_ready")
        conv_step = sem("conv_step")
        conv_ready = sem("conv_ready")
        u_ready = sem("u_ready")
        dt_ps = sem("dt_ps")
        bc_ps = sem("bc_ps")
        dt_x_ready = sem("dt_x_ready")
        bc_p1_ready = sem("bc_p1_ready")
        bc_r1_ready = sem("bc_r1_ready")
        bc_p2_ready = sem("bc_p2_ready")
        bc_parts_ready = sem("bc_parts_ready")
        dt_abs_ready = sem("dt_abs_ready")
        dt_z_ready = sem("dt_z_ready")
        dt_w_ready = sem("dt_w_ready")
        dt_ln_ready = sem("dt_ln_ready")
        dt_step = sem("dt_step")
        dt_ready = sem("dt_ready")
        dtu_ready = sem("dtu_ready")
        expA_ready = sem("expA_ready")
        negA_ready = sem("negA_ready")
        b_bc_ready = sem("b_bc_ready")
        c_bc_ready = sem("c_bc_ready")
        b_bc_used = sem("b_bc_used")
        dBu_ready = sem("dBu_ready")
        g_ready = sem("g_ready")
        dA_ready = sem("dA_ready")
        scan_done = sem("scan_done")
        carry_done = sem("carry_done")
        y_added = sem("y_added")
        y_seeded = sem("y_seeded")
        yv_ready = sem("yv_ready")
        w2_ps = sem("w2_ps")
        w2_o_ready = sem("w2_o_ready")

        thr_count_done = sem("thr_count_done")
        qk_ps, qk_raw, rot_ps = sem("qk_ps"), sem("qk_raw"), sem("rot_ps")
        tables_in = sem("tables_in")
        cos_ready, sin_ready, roped = sem("cos_ready"), sem("sin_ready"), sem("roped")
        hi_ready, rest_ready, mid_ready, lo_ready = (sem(n) for n in ("hi_ready", "rest_ready", "mid_ready", "lo_ready"))
        parts_stored = sem("parts_stored")
        stack_step, stacks_clear = sem("stack_step"), sem("stacks_clear")
        stack_in = [sem(f"stack_in{u}") for u in range(UN)]
        av_ps, v_pad, v_all_ready, v_head_ready = sem("av_ps"), sem("v_pad"), sem("v_all_ready"), sem("v_head_ready")
        s1_ps, s1_read, row_copied, max_step, max_parts_ready = (sem(n) for n in ("s1_ps", "s1_read", "row_copied", "max_step", "max_parts_ready"))
        s2_ps, p_ready, pv_done, o_copied = (sem(n) for n in ("s2_ps", "p_ready", "pv_done", "o_copied"))
        o_stored = [sem(f"o_stored{k}") for k in range(2)]
        o_in, inv_ready, inv_ps = (sem(n) for n in ("o_in", "inv_ready", "inv_ps"))
        attn_ready, wo_ps, wo_o_ready = sem("attn_ready"), sem("wo_ps"), sem("wo_o_ready")
        names = ["logits_ready", "route_step", "exp_ready", "wide_ready", "rep_ps", "rep_ready", "thr_step",
                 "thr_counted", "gates_final", "gates_stored", "hid_ps", "hid_ready", "out_ps", "out_gated", "acc_done"]
        ms = []
        for layer in range(2):
            m = {n: sem(f"l{layer}_{n}") for n in names}
            m["weights_in"] = [sem(f"l{layer}_weights_in{k}") for k in range(2)]
            m["gates_in"] = [sem(f"l{layer}_gates_in{k}") for k in range(2)]
            ms.append(m)

        block = ctx.enter_context(nc.Block())

        def c_bank(hf, k):
            return 2 if k == 0 else (6, 4)[hf]

        def chunk(t, c):
            return t[:, c * C:(c + 1) * C]

        def half(t, hf):
            return t[:, hf * HALF:(hf + 1) * HALF]

        @block.sync
        def _(sp):
            sp.dma_start(cols[:], cols_in).then_inc(params_in, 16)
            sp.dma_start(mats[:], mats_in).then_inc(params_in, 16)
            sp.dma_start(bcsel_f[:], bcsel_in).then_inc(params_in, 16)
            for c in range(NC):
                sp.dma_start(chunk(xT, c), chunk(xT_in, c)).then_inc(x_in[c], 16)
            sp.dma_start(router[:], router_in).then_inc(router_loaded, 16)
            sp.dma_start(digits[:], digits_in).then_inc(router_loaded, 16)

            def moe(layer):
                m = ms[layer]
                w1_in, w2_in = moe_in[layer][:2]

                def weights(e, k):
                    at = bass.ds(e, 1)
                    sp.dma_start(w1s[:, k, :], w1_in[at].rearrange("o p f -> (o p) f")).then_inc(m["weights_in"][k], 16)
                    sp.dma_start(w2s[:, k, :, :], w2_in[at].rearrange("o p c d -> (o p) c d")).then_inc(m["weights_in"][k], 16)
                    if layer == 0:
                        b1_in, b2_in = moe_in[layer][2:]
                        sp.dma_start(b1s[:, k, :], b1_in[at].rearrange("o p c -> (o p) c")).then_inc(m["weights_in"][k], 16)
                        sp.dma_start(b2s[:, k, :], b2_in[at].rearrange("o p c -> (o p) c")).then_inc(m["weights_in"][k], 16)

                def gates(e, k):
                    sp.dma_start(gate_bc[:, k, :], gates_dram[layer][bass.ds(e, 1)].rearrange("o t -> (o t)").partition_broadcast(128)).then_inc(m["gates_in"][k], 16)

                if layer:
                    sp.wait_ge(ms[0]["out_gated"], 2 + NE * NC)
                for k in range(2):
                    weights(k, k)
                sp.wait_ge(m["rep_ready"] if layer else m["gates_final"], 1)
                final = gates_rep if layer else gate_valid
                for e in range(NE):
                    sp.dma_start(gates_dram[layer][e:e + 1, :], final[REP * e:REP * e + 1, :]).then_inc(m["gates_stored"], 16)
                sp.wait_ge(m["gates_stored"], 16 * NE)
                for k in range(2):
                    gates(k, k)
                with sp.Fori(1, NE // 2) as i:
                    for k in range(2):
                        sp.wait_ge(m["out_gated"], i * 2 * NC + (NC * (k - 1) + 2))
                        weights(i * 2 + k, k)
                        gates(i * 2 + k, k)

            def attention():
                sp.wait_ge(ln_in_ready, 3 * NC)
                sp.dma_start(cosT[:], cos_in).then_inc(tables_in, 16)
                sp.dma_start(sinT[:], sin_in).then_inc(tables_in, 16)
                sp.dma_start(spread_sums[:], spread_in).then_inc(tables_in, 16)
                for hf in range(2):
                    sp.wait_ge(lo_ready, 4 * hf + 4)
                    sp.wait_ge(mid_ready, 4 * hf + 4)
                    for j in range(2):
                        at = slice(hf * HALF, (hf + 1) * HALF)
                        sp.dma_start(parts_dram[j][:, :, at], qk_parts[j][:, :, at]).then_inc(parts_stored, 16)
                sp.wait_ge(parts_stored, 64)
                sp.wait_ge(stacks_clear, 1)

                def stack(h, u):
                    rows = bass.ds(h * HD, HD)
                    q, k = q_stack[:, u, :], k_stack[:, u, :]
                    sp.dma_start(q[0:SHIFT].bitcast(F32), zero_in).then_inc(stack_in[u], 16)
                    for a in range(3):
                        lo = SHIFT + a * GROUP
                        sp.dma_start(q[lo:lo + GROUP], parts_dram[0][rows].rearrange("i b t -> (i b) t")).then_inc(stack_in[u], 16)
                        for b in range(3):
                            sp.dma_start(k[lo + b:lo + GROUP:3], parts_dram[1][rows, a, :]).then_inc(stack_in[u], 16)

                def store(u, sums_at, o_at):
                    sp.dma_start(sums_at, o_sb[HD:128:32, u % 2, :]).then_inc(o_stored[u % 2], 16)
                    for j in range(NC):
                        sp.dma_start(o_at(j), o_sb[32 * j:32 * j + HD, u % 2, :]).then_inc(o_stored[u % 2], 16)

                for u in range(UN):
                    stack(u, u)
                with sp.Fori(0, NH // UN - 1) as i:
                    for u in range(UN):
                        h = i * UN + u
                        sp.wait_ge(o_copied, h + 2)
                        store(u, sums_dram[bass.ds(h, 1)].rearrange("o j t -> (o j) t"), lambda j: o_dram[bass.ds(h * HD, HD), j, :])
                        sp.wait_ge(s2_ps, h * 2 * KT + 2 * KT)
                        stack(h + UN, u)
                for u in range(UN):
                    h = NH - UN + u
                    sp.wait_ge(o_copied, h + 2)
                    if u == 0:
                        for k in range(2):
                            sp.wait_ge(o_stored[k], 16 * STORES * (1 + h // 2))
                        sp.dma_start(sums[0:h * HD, :], sums_dram[0:h].rearrange("h j t -> (h j t)").rearrange("(p t) -> p t", t=SPAN)).then_inc(o_in, 16)
                        sp.dma_start(attnT[0:h * HD, :], o_dram[0:h * HD].rearrange("r j t -> r (j t)")).then_inc(o_in, 16)
                    at = slice(h * HD, (h + 1) * HD)
                    store(u, sums[at, :], lambda j: attnT[at, j * C:(j + 1) * C])

            moe(0)
            attention()
            moe(1)
            sp.wait_ge(ln_in_ready, 5 * NC)
            sp.dma_start(out, xT[:]).then_inc(out_done, 16)
            sp.wait_ge(out_done, 16)

        @block.tensor
        def _(pe):
            mm = nc.tensor.matmul

            def modulation():
                pe.wait_ge(wmod_loaded, 16)
                pe.wait_ge(silu_c_ready, 1)
                for j in range(12):
                    i = mm(psum[:, 7, j:j + 1], wmod[:, j, :], silu_c[:, j // 6:j // 6 + 1],
                           start=True, stop=True)
                i.then_inc(mod_ps_ready, 1)

            def layer_norm(k, src):
                def mean(c):
                    n = NC * k + c
                    if k == 0:
                        pe.wait_ge(x_in[c], 16)
                    else:
                        pe.wait_ge(ln_in_ready, NC * (k - 1) + c + 1)
                    if n >= 2:
                        pe.wait_ge(ln_xc_ready, n - 1)
                    mm(psum[:, c % 2, :], mat("mean"), chunk(src, c), start=True, stop=True).then_inc(ln_mean_ready, 1)

                def var(c):
                    n = NC * k + c
                    pe.wait_ge(ln_sq_ready, n + 1)
                    if n >= 2:
                        pe.wait_ge(ln_xn_ready, n - 1)
                    for t in range(TPC):
                        i = mm(psum[:, 2 + c % 2, t:t + 1], ln_sq[:, c % 2, t * 128:(t + 1) * 128], mat("mean")[:, 0:1],
                               start=True, stop=True)
                    i.then_inc(ln_var_ready, 1)

                def spread_rstd(c):
                    n = NC * k + c
                    pe.wait_ge(ln_rstd_ready, n + 1)
                    for t in range(TPC):
                        i = mm(psum[:, 2 + c % 2, t * 128:(t + 1) * 128],
                               ln_rstd[:, c % 2, t:t + 1].to_broadcast([128, 128]), mat("ident"), start=True, stop=True)
                    i.then_inc(ln_bc_ready, 1)

                mean(0)
                for c in range(NC):
                    if c + 1 < NC:
                        mean(c + 1)
                    var(c)
                    spread_rstd(c)

            def ssm_inputs():
                for c in range(NC):
                    pe.wait_ge(normed_ready, c + 1)
                    if c >= 2:
                        pe.wait_ge(x1_ready, c - 1)
                    mm(psum[:, 4 + c % 2, :], mat("w1"), chunk(normT, c), start=True, stop=True).then_inc(x1_ps, 1)
                    if c >= 2:
                        pe.wait_ge(v_ready, c - 1)
                    mm(psum[:, 6 + c % 2, :], mat("v1"), chunk(normT, c), start=True, stop=True).then_inc(v_ps, 1)
                pe.wait_ge(x1_ready, NC)
                pe.wait_ge(v_ready, NC)
                pe.wait_ge(ln_xn_ready, 2 * NC)
                for c in range(NC):
                    pe.wait_ge(u_ready, c + 1)
                    mm(psum[:, c, :], mat("W_dt"), chunk(uT, c), start=True, stop=True).then_inc(dt_ps, 1)
                    mm(psum[:, 4 + c, :], mat("W_BC"), chunk(uT, c), start=True, stop=True).then_inc(bc_ps, 1)

            def ssm_scan():
                def spread(bank, hf, column, done):
                    for j in range(2):
                        at = hf * HALF + j * C
                        i = mm(psum[:, bank + j, :], bcsel[:, bass.ds(column, 1)].to_broadcast([128, 128]),
                               bc_parts[:, at:at + C], start=True, stop=True)
                    i.then_inc(done, 1)

                def spread_b(hf, n, column):
                    pe.wait_ge(b_bc_used, n + 1)
                    spread(0, hf, column, b_bc_ready)

                def spread_c(hf, n, k, column):
                    pe.wait_ge(g_ready, n + 1)
                    spread(c_bank(hf, k), hf, column + NS, c_bc_ready)

                def add_y(hf, n, slot, last):
                    pe.wait_ge(g_ready, n + 3)
                    for j in range(2):
                        i = mm(psum[:, 4 + 2 * hf + j, :], mat("ident"), ssm_g[:, slot, j * C:(j + 1) * C],
                               start=False, stop=last, skip_group_check=True)
                    i.then_inc(y_added, 1)

                def state(hf, i, k, first=False, last=False):
                    n = i * 2 + (hf * NS + k)
                    column = i * 2 + k
                    spread_c(hf, n, k, column)
                    if not last:
                        spread_b(hf, n + 1, column + 1)
                    elif hf == 0:
                        spread_b(1, n + 1, 0)
                    if not first:
                        add_y(hf, n - 1, 1 - k, False)
                    if last:
                        add_y(hf, n, k, True)

                pe.wait_ge(bc_parts_ready, 2)
                pe.wait_ge(dt_x_ready, 2)
                pe.wait_ge(bcsel_ready, 1)
                pe.wait_ge(diag_ready, 1)
                spread_b(0, 0, 0)
                for hf in range(2):
                    for j in range(2):
                        i = mm(psum[:, 4 + 2 * hf + j, :], diag_skip[:], chunk(uT, 2 * hf + j),
                               start=True, stop=False, skip_group_check=True)
                    i.then_inc(y_seeded, 1)
                    state(hf, 0, 0, first=True)
                    if hf:
                        pe.wait_ge(yv_ready, 1)
                    state(hf, 0, 1)
                    with pe.Fori(1, NS // 2 - 1) as i:
                        for k in range(2):
                            state(hf, i, k)
                    state(hf, NS // 2 - 1, 0)
                    state(hf, NS // 2 - 1, 1, last=True)

            def ssm_out():
                for c in range(NC):
                    pe.wait_ge(yv_ready, c // 2 + 1)
                    if c == 0:
                        pe.wait_ge(g_ready, 2 * NS + 2)
                    mm(psum[:, c, :], mat("w2"), chunk(yvT, c), start=True, stop=True).then_inc(w2_ps, 1)

            def route(layer, done):
                m = ms[layer]
                pe.wait_ge(router_loaded, 32)
                for t in range(TILES):
                    if t % TPC == 0:
                        pe.wait_ge(normed_ready, done + t // TPC + 1)
                    i = mm(psum[:, 4, t * NE:(t + 1) * NE], normT[:, t * 128:(t + 1) * 128], router_w[layer],
                           start=True, stop=True)
                i.then_inc(m["logits_ready"], 1)
                pe.wait_ge(m["wide_ready"], 1)
                pe.wait_ge(ln_xn_ready, done + 2 * NC)
                for t in range(TILES):
                    i = mm(psum[:, t // TPC, (t % TPC) * 128:(t % TPC + 1) * 128],
                           ln_xc[:, t * 128:(t + 1) * 128], mat("ident"), start=True, stop=True)
                i.then_inc(m["rep_ps"], 1)
                if layer == 0:
                    with pe.Fori(0, ROUNDS) as r:
                        pe.wait_ge(m["thr_step"], r * 6 + 3)
                        mm(psum[:, 5, 0:1], mat("group"), thr_f["keep"][:], start=True, stop=True).then_inc(m["thr_counted"], 1)

            def experts(layer):
                m = ms[layer]
                pe.wait_ge(m["rep_ready"], 1)
                pe.sem_inc(m["out_ps"], 2)

                def up(i, k, tb):
                    n = i * 2 * NC + (k * NC + tb)
                    if tb == 0:
                        pe.wait_ge(m["weights_in"][k], (i + 1) * (64 if layer == 0 else 32))
                    for hc in range(HC):
                        pe.wait_ge(m["hid_ready"], n * HC + (hc + 1))
                        mm(psum[:, hc, :], w1s[:, k, hc * 128:(hc + 1) * 128], chunk(normT, tb),
                           start=True, stop=True).then_inc(m["hid_ps"], 1)

                def down(i, k, tb):
                    n = i * 2 * NC + (k * NC + tb)
                    pe.wait_ge(m["hid_ready"], n * HC + 2 * HC)
                    pe.wait_ge(m["out_gated"], n + 1)
                    for hc in range(HC):
                        j = mm(psum[:, 4 + tb % 2, :], w2s[:, k, hc, :], hidden[:, tb % 2, hc, :],
                               start=hc == 0, stop=hc == HC - 1)
                    j.then_inc(m["out_ps"], 1)

                def pair(i, last=False):
                    for q in range(2 * NC):
                        if q + 1 < 2 * NC:
                            up(i, (q + 1) // NC, (q + 1) % NC)
                        elif not last:
                            up(i + 1, 0, 0)
                        down(i, q // NC, q % NC)

                up(0, 0, 0)
                with pe.Fori(0, NE // 2 - 1) as i:
                    pair(i)
                pair(NE // 2 - 1, last=True)

            def attention_inputs():
                done = 2 * NC
                pe.wait_ge(ln_xn_ready, 4 * NC)

                def project(m):
                    c, j = m // 2, m % 2
                    pe.wait_ge(normed_ready, done + c + 1)
                    if m >= 2:
                        pe.wait_ge(qk_raw, m - 1)
                    mm(psum[:, 4 + j, :], mat(("WqT", "WkT")[j]), chunk(normT, c), start=True, stop=True).then_inc(qk_ps, 1)

                def rotate(m):
                    c, j = m // 2, m % 2
                    pe.wait_ge(qk_raw, m + 1)
                    if m >= 2:
                        pe.wait_ge(sin_ready, m - 1)
                    mm(psum[:, 6 + j, :], mat("rotate"), chunk(qkT[j], c), start=True, stop=True).then_inc(rot_ps, 1)

                project(0)
                for m in range(2 * NC):
                    if m + 1 < 2 * NC:
                        project(m + 1)
                    rotate(m)
                for t in range(TILES):
                    mm(psum[:, t // TPC, (t % TPC) * 128:(t % TPC + 1) * 128], normT[:, t * 128:(t + 1) * 128], mat("WvT"),
                       start=True, stop=True).then_inc(av_ps, 1)

            def attention():
                pe.wait_ge(v_all_ready, TILES)
                pe.wait_ge(sin_ready, 2 * NC)
                pe.sem_inc(pv_done, 4)

                def ring(hs, p):
                    before = p - RING if p >= RING else (SN - 2, SN - 1, SN - 3)[p]
                    heads = 0 if p >= RING else 1
                    if STREAM[before][1] == "row":
                        pe.wait_ge(row_copied, hs * ROWS + (STREAM[before][2] + 1 + ROWS * (1 - heads)))
                    else:
                        qt, c = STREAM[before][2]
                        pe.wait_ge(s1_read, hs * SCORES + (qt * NC + c + 1 + RING - SCORES * heads))
                    return psum[:, 4 + p % RING, :]

                def maxima(hs, u, p, turn=0):
                    step, kind, x = STREAM[p]
                    if p == 0:
                        pe.wait_ge(stack_in[u], turn * (16 * STACK_LOADS) + 16 * STACK_LOADS)
                    bank = ring(hs, p)
                    if kind == "scores":
                        qt, c = x
                        i = mm(bank, q_stack[:, u, qt * 128:(qt + 1) * 128], k_stack[:, u, c * C:(c + 1) * C], start=True, stop=True)
                    else:
                        pe.wait_ge(max_parts_ready, hs * 4 + (x + 1))
                        for j in range(4):
                            i = mm(bank[0:SHIFT, j * 128:(j + 1) * 128], max_parts[:, x, j, :], ident_b[:], start=True, stop=True)
                    i.then_inc(s1_ps, 1)

                def scores(h, u, t):
                    if t == 0:
                        pe.wait_ge(row_copied, h * ROWS + 2 * ROWS)
                    pe.wait_ge(p_ready, h * 2 * KT + (t + 1))
                    kt, b = t // 2, t % 2
                    for j in range(2):
                        at = b * HALF + j * C
                        i = mm(psum[:, 2 * b + j, :], k_stack[:, u, kt * 128:(kt + 1) * 128], q_stack[:, u, at:at + C], start=True, stop=True)
                    i.then_inc(s2_ps, 1)

                def values(h, u, kt):
                    if kt == 0:
                        pe.wait_ge(v_head_ready, h + 1)
                        pe.wait_ge(o_copied, h + 1)
                    pe.wait_ge(p_ready, h * 2 * KT + (2 * kt + 4))
                    for j in range(NC):
                        i = mm(psum[32 * j:32 * j + VM, 7, :], v_head[:, u, kt, :], probs[:, kt % 4, j * C:(j + 1) * C],
                               start=kt == 0, stop=kt == KT - 1)
                    i.then_inc(pv_done, 1)

                def head(h, u, turn, following=NH):
                    for kt in range(KT):
                        s = kt + AHEAD
                        mine = [(1, p) for p in range(SN) if STREAM[p][0] == s]
                        if s >= KT:
                            mine += [(2, p) for p in range(SN) if STREAM[p][0] == s - KT]
                        mine = [(d, p) for d, p in mine if d <= following]

                        def take(n):
                            for d, p in mine[:n]:
                                maxima(h + d, (u + d) % UN, p, turn + (u + d) // UN)
                            del mine[:n]

                        late = s == KT
                        scores(h, u, 2 * kt)
                        take(0 if late else 1)
                        scores(h, u, 2 * kt + 1)
                        take(0 if late else 1)
                        if kt:
                            values(h, u, kt - 1)
                        take(len(mine))
                    values(h, u, KT - 1)

                for p in range(SN):
                    maxima(0, 0, p)
                for p in range(SN):
                    if STREAM[p][0] < AHEAD:
                        maxima(1, 1, p)
                with pe.Fori(0, NH // UN - 1) as i:
                    for u in range(UN):
                        head(i * UN + u, u, i)
                for u in range(UN):
                    head(NH - UN + u, u, NH // UN - 1, following=UN - 1 - u)

            def attention_out():
                pe.wait_ge(inv_ready, 1)
                pe.wait_ge(p_ready, 2 + 2 * KT * NH)
                for i in range(HD):
                    j = mm(banks(0, 4)[:, i * SPAN:(i + 1) * SPAN], spread_sums[:, i, :], sums[:], start=True, stop=True)
                    if (i + 1) * SPAN % C == 0:
                        j.then_inc(inv_ps, 1)
                pe.wait_ge(o_copied, 1 + NH)
                for c in range(NC):
                    pe.wait_ge(attn_ready, c + 1)
                    mm(psum[:, 4 + c, :], mat("WoT"), chunk(attnT, c), start=True, stop=True).then_inc(wo_ps, 1)

            pe.wait_ge(params_in, 48)
            modulation()
            layer_norm(0, xT)
            layer_norm(1, h0T)
            ssm_inputs()
            ssm_scan()
            ssm_out()
            layer_norm(2, xT)
            route(0, NC)
            experts(0)
            layer_norm(3, xT)
            attention_inputs()
            attention()
            attention_out()
            layer_norm(4, xT)
            route(1, 3 * NC)
            experts(1)

        @block.scalar
        def _(act):
            f = nc.scalar.activation

            def modulation():
                act.dma_start(wmod[:], wmod_in).then_inc(wmod_loaded, 16)
                act.wait_ge(params_in, 48)
                f(silu_c[:], cols[:, COL["c0"]:COL["c0"] + 2], ACT.Silu).then_inc(silu_c_ready, 1)

            def layer_norm(k):
                def square(c):
                    n = NC * k + c
                    act.wait_ge(ln_xc_ready, n + 1)
                    if n >= 2:
                        act.wait_ge(ln_var_ready, n - 1)
                    f(ln_sq[:, c % 2, :], chunk(ln_xc, c), ACT.Square).then_inc(ln_sq_ready, 1)

                def std(c):
                    n = NC * k + c
                    act.wait_ge(ln_var_ready, n + 1)
                    if n >= 2:
                        act.wait_ge(ln_rstd_ready, n - 1)
                    f(ln_std[:, c % 2, :], psum[:, 2 + c % 2, 0:TPC], ACT.Sqrt, bias=eps_col[:]).then_inc(ln_std_ready, 1)

                square(0)
                for c in range(NC):
                    if c + 1 < NC:
                        square(c + 1)
                    std(c)

            def ssm_inputs():
                for c in range(NC):
                    act.wait_ge(x1_ps, c + 1)
                    f(x1pad[:, 1 + c * C:1 + (c + 1) * C], psum[:, 4 + c % 2, :], ACT.Identity,
                      bias=col("w1_b")).then_inc(x1_ready, 1)
                    act.wait_ge(v_ps, c + 1)
                    f(chunk(vT, c), psum[:, 6 + c % 2, :], ACT.Silu, bias=col("v1_b")).then_inc(v_ready, 1)
                for c in range(NC):
                    act.wait_ge(conv_ready, c + 1)
                    f(chunk(uT, c), chunk(conv_y, c), ACT.Silu).then_inc(u_ready, 1)
                f(expA[:], cols[:, A_LOG:A_LOG + NS], ACT.Exp).then_inc(expA_ready, 1)
                for hf in range(2):
                    act.wait_ge(dt_ps, 2 * hf + 2)
                    f(half(dt_x, hf), banks(2 * hf, 2), ACT.Identity, bias=col("b_dt")).then_inc(dt_x_ready, 1)
                    act.wait_ge(dt_x_ready, hf + 1)
                    f(half(dt_abs, hf), half(dt_x, hf), ACT.Abs).then_inc(dt_abs_ready, 1)
                    act.wait_ge(bc_ps, 2 * hf + 2)
                    f(half(bc_p1, hf), banks(4 + 2 * hf, 2), ACT.Identity).then_inc(bc_p1_ready, 1)
                for hf in range(2):
                    act.wait_ge(dt_abs_ready, hf + 1)
                    f(half(dt_z, hf), half(dt_abs, hf), ACT.Exp, scale=-1.0).then_inc(dt_z_ready, 1)
                    act.wait_ge(bc_r1_ready, hf + 1)
                    f(half(bc_p2, hf), half(bc_r1, hf), ACT.Identity).then_inc(bc_p2_ready, 1)
                for hf in range(2):
                    act.wait_ge(dt_w_ready, hf + 1)
                    f(half(dt_ln, hf), half(dt_w, hf), ACT.Ln).then_inc(dt_ln_ready, 1)

            def ssm_scan():
                act.wait_ge(negA_ready, 1)
                for hf in range(2):
                    act.wait_ge(dt_ready, hf + 1)
                    with act.Fori(0, NS // 2) as i:
                        for k in range(2):
                            n = i * 2 + (hf * NS + k)
                            act.wait_ge(b_bc_ready, n + 1)
                            act.wait_ge(dBu_ready, n + 1)
                            f(ssm_b[:, k, :], banks(0, 2), ACT.Identity).then_inc(b_bc_used, 1)
                            act.wait_ge(scan_done, n + 1)
                            f(ssm_dA[:, k, :], half(dtT, hf), ACT.Exp,
                              scale=negA[:, bass.ds(i * 2 + k, 1)]).then_inc(dA_ready, 1)

            def ssm_out():
                act.wait_ge(mod_ready, 2)
                for c in range(NC):
                    act.wait_ge(w2_ps, c + 1)
                    if c >= 2:
                        act.wait_ge(ln_in_ready, NC + c - 1)
                    f(proj_o[:, c % 2, :], psum[:, c, :], ACT.Identity, bias=gated_w2b[:],
                      scale=modc(0, GA)).then_inc(w2_o_ready, 1)

            def route(layer):
                m = ms[layer]
                act.wait_ge(m["route_step"], 3)
                f(rt["prob"][:], rt["logit"][:], ACT.Exp).then_inc(m["exp_ready"], 1)
                act.wait_ge(m["rep_ps"], 1)
                f(gates_rep[:], banks(0, 4), ACT.Identity).then_inc(m["rep_ready"], 1)

            def experts(layer):
                m = ms[layer]
                act.sem_inc(m["hid_ready"], HC)
                with act.Fori(0, NE // 2) as i:
                    for k in range(2):
                        for tb in range(NC):
                            n = i * 2 * NC + (k * NC + tb)
                            act.wait_ge(m["out_ps"], n + 1)
                            for hc in range(HC):
                                act.wait_ge(m["hid_ps"], n * HC + (hc + 1))
                                if layer == 0:
                                    i_ = f(hidden[:, tb % 2, hc, :], psum[:, hc, :], ACT.Silu, bias=b1s[:, k, hc:hc + 1])
                                else:
                                    i_ = f(hidden[:, tb % 2, hc, :], psum[:, hc, :], ACT.Gelu)
                                i_.then_inc(m["hid_ready"], 1)

            def attention_inputs():
                def raw(m):
                    c, j = m // 2, m % 2
                    act.wait_ge(qk_ps, m + 1)
                    f(chunk(qkT[j], c), psum[:, 4 + j, :], ACT.Identity, bias=col(("bq", "bk")[j])).then_inc(qk_raw, 1)

                def hi(m):
                    c, j = m // 2, m % 2
                    act.wait_ge(roped, m + 1)
                    f(chunk(qk_parts[j][:, 0, :], c), chunk(qkT[j], c), ACT.Identity).then_inc(hi_ready, 1)

                def mid(m):
                    c, j = m // 2, m % 2
                    act.wait_ge(rest_ready, m + 1)
                    f(chunk(qk_parts[j][:, 1, :], c), qk_rest[:, m % 2, :], ACT.Identity).then_inc(mid_ready, 1)

                raw(0)
                raw(1)
                for m in range(2 * NC + 1):
                    if m + 2 < 2 * NC:
                        raw(m + 2)
                    if m < 2 * NC:
                        hi(m)
                    if m:
                        mid(m - 1)

            def attention():
                act.sem_inc(p_ready, 2)
                act.sem_inc(o_copied, 1)
                for k in range(2):
                    act.sem_inc(o_stored[k], 16 * STORES)

                def row(hs, u, p):
                    act.wait_ge(s1_ps, hs * SN + (p + 1))
                    x = STREAM[p][2]
                    f(q_stack[0:SHIFT, u, x * C:(x + 1) * C], psum[0:SHIFT, 4 + p % RING, :], ACT.Identity).then_inc(row_copied, 1)

                def head(h, u, turn, following=True):
                    for t in range(2 * KT):
                        kt, b = t // 2, t % 2
                        act.wait_ge(s2_ps, h * 2 * KT + (t + 1))
                        if b == 0:
                            act.wait_ge(pv_done, h * KT + (kt + 1))
                        f(probs[:, kt % 4, b * HALF:(b + 1) * HALF], banks(2 * b, 2), ACT.Exp, scale=SCALE).then_inc(p_ready, 1)
                        for p in range(SN):
                            at = 2 * (STREAM[p][0] - AHEAD) + (1 if STREAM[p][0] == KT else 2)
                            if following and STREAM[p][1] == "row" and t == at:
                                row(h + 1, (u + 1) % UN, p)
                    act.wait_ge(pv_done, h * KT + (KT + 4))
                    act.wait_ge(o_stored[u % 2], turn * (16 * STORES * UN // 2) + 16 * STORES * (u // 2 + 1))
                    f(o_sb[:, u % 2, :], psum[:, 7, :], ACT.Identity).then_inc(o_copied, 1)

                act.sem_inc(row_copied, ROWS)
                for p in range(SN):
                    if STREAM[p][1] == "row":
                        row(0, 0, p)
                with act.Fori(0, NH // UN - 1) as i:
                    for u in range(UN):
                        head(i * UN + u, u, i)
                for u in range(UN):
                    head(NH - UN + u, u, NH // UN - 1, following=u < UN - 1)

            def attention_out():
                for c in range(NC):
                    act.wait_ge(wo_ps, c + 1)
                    if c >= 2:
                        act.wait_ge(ln_in_ready, 3 * NC + c - 1)
                    f(proj_o[:, c % 2, :], psum[:, 4 + c, :], ACT.Identity, bias=gated_bo[:],
                      scale=modc(1, GA)).then_inc(wo_o_ready, 1)

            modulation()
            layer_norm(0)
            layer_norm(1)
            ssm_inputs()
            ssm_scan()
            ssm_out()
            layer_norm(2)
            route(0)
            experts(0)
            layer_norm(3)
            attention_inputs()
            attention()
            attention_out()
            layer_norm(4)
            route(1)
            experts(1)

        @block.gpsimd
        def _(pool):
            g = nc.gpsimd

            def ssm_scan():
                pool.wait_ge(dtu_ready, 2)
                for hf in range(2):
                    with pool.Fori(0, NS // 2) as i:
                        for k in range(2):
                            n = i * 2 + (hf * NS + k)
                            pool.wait_ge(b_bc_used, n + 2)
                            pool.wait_ge(scan_done, n + 1)
                            g.tensor_tensor(ssm_dBu[:, k, :], half(dtuT, hf), ssm_b[:, k, :], ALU.mult).then_inc(dBu_ready, 1)

            def experts(layer):
                m = ms[layer]
                pool.sem_inc(m["acc_done"], 1)
                pool.wait_ge(ln_in_ready, 2 * NC * (layer + 1))
                g.memset(moe_acc[:], 0.0).then_inc(m["acc_done"], 1)
                with pool.Fori(0, NE // 2) as i:
                    for k in range(2):
                        for tb in range(NC):
                            n = i * 2 * NC + (k * NC + tb)
                            pool.wait_ge(m["out_gated"], n + 3)
                            pool.wait_ge(m["acc_done"], n + 2)
                            g.tensor_tensor(chunk(moe_acc, tb), chunk(moe_acc, tb), gated[:, tb % 2, :],
                                            ALU.add).then_inc(m["acc_done"], 1)

            def attention_inputs():
                pool.wait_ge(ln_in_ready, 3 * NC)
                for t in (q_stack, k_stack):
                    g.memset(t[:], 0.0).then_inc(stack_step, 1)
                pool.wait_ge(stack_step, 2)
                g.memset(k_stack[0:SHIFT], -1.0).then_inc(stacks_clear, 1)
                pool.wait_ge(tables_in, 48)
                for m in range(2 * NC):
                    c, j = m // 2, m % 2
                    pool.wait_ge(qk_raw, m + 1)
                    if m >= 2:
                        pool.wait_ge(roped, m - 1)
                    g.tensor_tensor(rope_cos[:, m % 2, :], chunk(qkT[j], c), chunk(cosT, c), ALU.mult).then_inc(cos_ready, 1)
                g.memset(v_head[:], 0.0).then_inc(v_pad, 1)
                g.memset(v_all[:, :, :, HD:HD + 1], 1.0).then_inc(v_pad, 1)

            def attention():
                pool.wait_ge(v_pad, 2)
                pool.wait_ge(v_all_ready, TILES)

                def head(h, u):
                    g.tensor_copy(v_head[:, u, :, 0:HD + 1], v_all[:, :, bass.ds(h, 1), :].rearrange("p k o d -> p k (o d)")).then_inc(v_head_ready, 1)

                for u in range(UN):
                    head(u, u)
                with pool.Fori(1, NH // UN) as i:
                    for u in range(UN):
                        pool.wait_ge(pv_done, i * (UN * KT) + (KT * (u - UN + 1) + 4))
                        head(i * UN + u, u)

            ssm_scan()
            experts(0)
            attention_inputs()
            attention()
            experts(1)

        @block.vector
        def _(dve):
            v = nc.vector

            def modulation():
                v.memset(eps_col[:], EPS).then_inc(misc_step, 1)
                v.memset(x1pad[:, 0:1], 0.0).then_inc(pad_ready, 1)
                v.memset(x1pad[:, L + 1:L + 2], 0.0).then_inc(pad_ready, 1)
                dve.wait_ge(params_in, 48)
                v.tensor_copy(ident_b[:], mat("ident")).then_inc(misc_step, 1)
                v.tensor_copy(bcsel[:], bcsel_f[:]).then_inc(bcsel_ready, 1)
                v.tensor_scalar(diag_skip[:], mat("ident"), col("D_skip"), None, ALU.mult).then_inc(diag_ready, 1)
                dve.wait_ge(mod_ps_ready, 1)
                v.tensor_copy(mod[:], psum[:, 7, 0:12]).then_inc(mod_step, 1)
                dve.wait_ge(mod_step, 1)
                gates = mod[:].rearrange("p (a b) -> p a b", b=3)[:, :, GA:GA + 1]
                scales = mod[:].rearrange("p (a b) -> p a b", b=3)[:, :, CA:CA + 1]
                size, sign = (t[:].rearrange("p (a b) -> p a b", b=1) for t in (gate_size, gate_sign))
                v.tensor_scalar(scales, scales, 1.0, None, ALU.add).then_inc(mod_step, 1)
                v.tensor_scalar(sign, gates, 0.0, 2.0, ALU.is_ge, ALU.mult).then_inc(mod_step, 1)
                dve.wait_ge(mod_step, 3)
                v.tensor_scalar(sign, sign, -1.0, None, ALU.add).then_inc(mod_step, 1)
                dve.wait_ge(mod_step, 4)
                v.tensor_tensor(size, gates, sign, ALU.mult).then_inc(mod_step, 1)
                dve.wait_ge(mod_step, 5)
                v.scalar_tensor_tensor(gates, size, 0.25, sign, ALU.max, ALU.mult).then_inc(mod_step, 1)
                dve.wait_ge(mod_step, 6)
                v.tensor_tensor(gated_bo[:], col("bo"), modc(1, GA), ALU.mult).then_inc(mod_ready, 1)
                v.tensor_tensor(gated_w2b[:], col("w2_b"), modc(0, GA), ALU.mult).then_inc(mod_ready, 1)

            def layer_norm(k, src, dst, scale, bias, ready):
                def centre(c):
                    n = NC * k + c
                    dve.wait_ge(ln_mean_ready, n + 1)
                    v.tensor_tensor(chunk(ln_xc, c), chunk(src, c), psum[:, c % 2, :], ALU.subtract).then_inc(ln_xc_ready, 1)

                def rstd(c):
                    n = NC * k + c
                    dve.wait_ge(ln_std_ready, n + 1)
                    v.reciprocal(ln_rstd[:, c % 2, :], ln_std[:, c % 2, :]).then_inc(ln_rstd_ready, 1)

                def scaled(c):
                    n = NC * k + c
                    s = c % 2
                    dve.wait_ge(ln_bc_ready, n + 1)
                    v.tensor_tensor(ln_xn[:, s, :], chunk(ln_xc, c), psum[:, 2 + s, :], ALU.mult).then_inc(ln_xn_ready, 1)
                    dve.wait_ge(ln_xn_ready, n + 1)
                    v.tensor_scalar(chunk(dst, c), ln_xn[:, s, :], scale, bias, ALU.mult, ALU.add).then_inc(ready, 1)

                centre(0)
                for c in range(NC):
                    if c + 1 < NC:
                        centre(c + 1)
                    rstd(c)
                    scaled(c)

            def ssm_inputs():
                dve.wait_ge(pad_ready, 2)
                for c in range(NC):
                    s, at = c % 2, c * C
                    dve.wait_ge(x1_ready, min(c + 2, NC))
                    v.tensor_scalar(conv_a[:, s, :], x1pad[:, at:at + C], col("conv0"), None, ALU.mult).then_inc(conv_step, 1)
                    dve.wait_ge(conv_step, 2 * c + 1)
                    v.scalar_tensor_tensor(conv_b[:, s, :], x1pad[:, at + 1:at + 1 + C], col("conv1"), conv_a[:, s, :],
                                           ALU.mult, ALU.add).then_inc(conv_step, 1)
                    dve.wait_ge(conv_step, 2 * c + 2)
                    v.scalar_tensor_tensor(chunk(conv_y, c), x1pad[:, at + 2:at + 2 + C], col("conv2"), conv_b[:, s, :],
                                           ALU.mult, ALU.add).then_inc(conv_ready, 1)
                dve.wait_ge(expA_ready, 1)
                v.tensor_scalar(negA[:], expA[:], -1.0, None, ALU.mult).then_inc(negA_ready, 1)
                for hf in range(2):
                    dve.wait_ge(bc_p1_ready, hf + 1)
                    v.scalar_tensor_tensor(half(bc_r1, hf), half(bc_p1, hf), col("part1"), banks(4 + 2 * hf, 2),
                                           ALU.mult, ALU.add).then_inc(bc_r1_ready, 1)
                for hf in range(2):
                    dve.wait_ge(dt_z_ready, hf + 1)
                    v.tensor_scalar(half(dt_w, hf), half(dt_z, hf), 1.0, None, ALU.add).then_inc(dt_w_ready, 1)
                    dve.wait_ge(bc_p2_ready, hf + 1)
                    v.scalar_tensor_tensor(half(bc_parts, hf), half(bc_p2, hf), col("part2"), half(bc_r1, hf),
                                           ALU.mult, ALU.add).then_inc(bc_parts_ready, 1)
                    dve.wait_ge(dt_w_ready, hf + 1)
                    v.scalar_tensor_tensor(half(dt_e, hf), half(dt_w, hf), 1.0, half(dt_z, hf),
                                           ALU.subtract, ALU.subtract).then_inc(dt_step, 1)
                    dve.wait_ge(dt_step, 2 * hf + 1)
                    dve.wait_ge(dt_ln_ready, hf + 1)
                    v.tensor_tensor(half(dt_r, hf), half(dt_ln, hf), half(dt_e, hf), ALU.subtract).then_inc(dt_step, 1)
                    dve.wait_ge(dt_step, 2 * hf + 2)
                    v.scalar_tensor_tensor(half(dtT, hf), half(dt_x, hf), 0.0, half(dt_r, hf),
                                           ALU.max, ALU.add).then_inc(dt_ready, 1)
                    dve.wait_ge(dt_ready, hf + 1)
                    v.tensor_tensor(half(dtuT, hf), half(dtT, hf), half(uT, hf), ALU.mult).then_inc(dtu_ready, 1)

            def ssm_scan():
                dve.wait_ge(dtu_ready, 2)
                dve.sem_inc(b_bc_used, 1)
                dve.sem_inc(g_ready, 2)
                dve.sem_inc(dBu_ready, 2)
                dve.sem_inc(scan_done, 2)
                dve.sem_inc(carry_done, 2)
                for hf in range(2):
                    with dve.Fori(0, NS // 2) as i:
                        for k in range(2):
                            n = i * 2 + (hf * NS + k)
                            at = bass.ds(i * 2 + k, 1)
                            dve.wait_ge(dA_ready, n + 1)
                            dve.wait_ge(dBu_ready, n + 3)
                            dve.wait_ge(g_ready, n + 1)
                            dve.wait_ge(carry_done, n + 1)
                            v.tensor_tensor_scan(ssm_h[:, k, :], ssm_dA[:, k, :], ssm_dBu[:, k, :],
                                                 ssm_carry[:, at] if hf else 0.0,
                                                 ALU.mult, ALU.add).then_inc(scan_done, 1)
                            dve.wait_ge(c_bc_ready, n + 1)
                            dve.wait_ge(scan_done, n + 3)
                            dve.wait_ge(y_added, n + 1)
                            v.tensor_tensor(ssm_g[:, k, :], ssm_h[:, k, :], banks(c_bank(hf, k), 2), ALU.mult).then_inc(g_ready, 1)
                            v.tensor_copy(ssm_carry[:, at], ssm_h[:, k, HALF - 1:HALF]).then_inc(carry_done, 1)
                    dve.wait_ge(y_added, 2 + NS * (hf + 1))
                    v.tensor_tensor(half(yvT, hf), banks(4 + 2 * hf, 2), half(vT, hf), ALU.mult).then_inc(yv_ready, 1)

            def residual(ready, base):
                for c in range(NC):
                    dve.wait_ge(ready, c + 1)
                    v.tensor_tensor(chunk(xT, c), chunk(xT, c), proj_o[:, c % 2, :], ALU.add).then_inc(ln_in_ready, 1)

            def route(layer):
                m = ms[layer]
                steps = [0]

                def step(i):
                    steps[0] += 1
                    i.then_inc(m["route_step"], 1)
                    dve.wait_ge(m["route_step"], steps[0])

                def wide(t):
                    return t[:].unsqueeze(2).to_broadcast([128, TILES, NE])

                def each(t):
                    return t.unsqueeze(1).to_broadcast([128, TILES, NE])

                logits = psum[:, 4, 0:TILES * NE].rearrange("p (t e) -> p t e", e=NE)
                dve.wait_ge(m["logits_ready"], 1)
                if layer == 0:
                    step(v.tensor_tensor(rt["logit"][:], logits, each(router_b), ALU.add))
                else:
                    step(v.tensor_copy(rt["logit"][:], logits))
                step(v.tensor_reduce(rs["max"][:], rt["logit"][:], AX.X, ALU.max))
                step(v.tensor_tensor(rt["logit"][:], rt["logit"][:], wide(rs["max"]), ALU.subtract))
                dve.wait_ge(m["exp_ready"], 1)
                step(v.tensor_reduce(rs["sum"][:], rt["prob"][:], AX.X, ALU.add))
                step(v.reciprocal(rs["inv"][:], rs["sum"][:]))
                step(v.tensor_tensor(rt["prob"][:], rt["prob"][:], wide(rs["inv"]), ALU.mult))

                def best(src, top, out):
                    step(v.tensor_reduce(rs[top][:], rt[src][:], AX.X, ALU.max))
                    step(v.tensor_tensor(rt["eq"][:], rt[src][:], wide(rs[top]), ALU.is_equal))
                    step(v.tensor_tensor(rt["eq"][:], rt["eq"][:], each(expert_no), ALU.mult))
                    step(v.tensor_reduce(rs["no"][:], rt["eq"][:], AX.X, ALU.min))
                    step(v.tensor_tensor(rt[out][:], wide(rs["no"]), each(expert_no), ALU.is_equal))

                best("prob", "top1", "best1")
                step(v.scalar_tensor_tensor(rt["rest"][:], rt["best1"][:], -4.0, rt["prob"][:], ALU.mult, ALU.add))
                best("rest", "top2", "best2")
                step(v.tensor_tensor(rt["best1"][:], rt["best1"][:], rt["best2"][:], ALU.add))
                step(v.tensor_tensor(rt["gate"][:], rt["best1"][:], rt["prob"][:], ALU.mult))
                if layer == 1:
                    step(v.tensor_tensor(rs["sum"][:], rs["top1"][:], rs["top2"][:], ALU.add))
                    step(v.reciprocal(rs["inv"][:], rs["sum"][:]))
                    step(v.tensor_tensor(rt["gate"][:], rt["gate"][:], wide(rs["inv"]), ALU.mult))
                v.tensor_copy(gate_wide, rt["gate"][:].unsqueeze(3).to_broadcast([128, TILES, NE, REP])).then_inc(m["wide_ready"], 1)

            def keep_capacity():
                m = ms[0]
                dve.wait_ge(m["rep_ready"], 1)
                v.memset(thr["low"][:], 0).then_inc(m["thr_step"], 1)
                with dve.Fori(0, ROUNDS) as r:
                    at = bass.ds(r, 1)
                    dve.wait_ge(m["thr_step"], r * 6 + 1)
                    v.tensor_tensor(thr["try"][:], thr["low"][:], digits[:, at], ALU.bitwise_or).then_inc(m["thr_step"], 1)
                    dve.wait_ge(m["thr_step"], r * 6 + 2)
                    v.tensor_scalar(gate_eq[:], gates_rep[:], thr["try"][:].bitcast(F32), None, ALU.is_ge,
                                    ALU.add, accum_out=thr_f["count"][:]).then_inc(thr_count_done, 1)
                    dve.wait_ge(thr_count_done, r + 1)
                    v.tensor_scalar(thr_f["keep"][:], thr_f["count"][:], CAP - 0.5, None, ALU.is_ge).then_inc(m["thr_step"], 1)
                    dve.wait_ge(m["thr_counted"], r + 1)
                    v.tensor_scalar(thr["add"][:], psum[:, 5, 0:1], -1.0, digit_size[:, at], ALU.add, ALU.mult).then_inc(m["thr_step"], 1)
                    dve.wait_ge(m["thr_step"], r * 6 + 4)
                    v.tensor_tensor(thr["low"][:], thr["low"][:], thr["add"][:], ALU.bitwise_or).then_inc(m["thr_step"], 3)
                low = thr["low"][:].bitcast(F32)
                base = [ROUNDS * 6 + 1]

                def step(i):
                    base[0] += 1
                    i.then_inc(m["thr_step"], 1)
                    dve.wait_ge(m["thr_step"], base[0])

                dve.wait_ge(m["thr_step"], base[0])
                step(v.tensor_scalar(gate_eq[:], gates_rep[:], low, None, ALU.is_gt, ALU.add, accum_out=thr_f["count"][:]))
                step(v.tensor_scalar(thr_f["quota"][:], thr_f["count"][:], -1.0, float(CAP), ALU.mult, ALU.add))
                step(v.tensor_scalar(gate_eq[:], gates_rep[:], low, None, ALU.is_equal))
                step(v.tensor_tensor_scan(gate_rank[:], gate_eq[:], gate_eq[:], 0.0, ALU.add, ALU.max))
                step(v.scalar_tensor_tensor(gate_eq[:], gate_rank[:], thr_f["quota"][:], gate_eq[:], ALU.is_le, ALU.mult))
                step(v.scalar_tensor_tensor(gate_eq[:], gates_rep[:], low, gate_eq[:], ALU.is_gt, ALU.add))
                v.tensor_tensor(gate_valid[:], gates_rep[:], gate_eq[:], ALU.mult).then_inc(m["gates_final"], 1)

            def experts(layer):
                m = ms[layer]
                dve.sem_inc(m["out_gated"], 2)
                with dve.Fori(0, NE // 2) as i:
                    for k in range(2):
                        dve.wait_ge(m["gates_in"][k], (i + 1) * 16)
                        for tb in range(NC):
                            n = i * 2 * NC + (k * NC + tb)
                            dve.wait_ge(m["out_ps"], n + 3)
                            dve.wait_ge(m["acc_done"], n + 1)
                            o, a, g = gated[:, tb % 2, :], psum[:, 4 + tb % 2, :], gate_bc[:, k, tb * C:(tb + 1) * C]
                            if layer == 0:
                                j = v.scalar_tensor_tensor(o, a, b2s[:, k, :], g, ALU.add, ALU.mult)
                            else:
                                j = v.tensor_tensor(o, a, g, ALU.mult)
                            j.then_inc(m["out_gated"], 1)
                for c in range(NC):
                    dve.wait_ge(m["acc_done"], 2 + NE * NC - (NC - 1 - c))
                    v.scalar_tensor_tensor(chunk(xT, c), chunk(moe_acc, c), modc(layer, GB), chunk(xT, c),
                                           ALU.mult, ALU.add).then_inc(ln_in_ready, 1)

            def attention_inputs():
                dve.wait_ge(tables_in, 48)

                def rope(m):
                    c, j = m // 2, m % 2
                    dve.wait_ge(rot_ps, m + 1)
                    v.tensor_tensor(rope_sin[:, m % 2, :], psum[:, 6 + j, :], chunk(sinT, c), ALU.mult).then_inc(sin_ready, 1)
                    dve.wait_ge(sin_ready, m + 1)
                    dve.wait_ge(cos_ready, m + 1)
                    v.tensor_tensor(chunk(qkT[j], c), rope_cos[:, m % 2, :], rope_sin[:, m % 2, :], ALU.add).then_inc(roped, 1)

                def rest(m):
                    c, j = m // 2, m % 2
                    if m >= 2:
                        dve.wait_ge(lo_ready, m - 1)
                    dve.wait_ge(hi_ready, m + 1)
                    dve.wait_ge(roped, m + 1)
                    v.tensor_tensor(qk_rest[:, m % 2, :], chunk(qkT[j], c), chunk(qk_parts[j][:, 0, :], c), ALU.subtract).then_inc(rest_ready, 1)

                def low(m):
                    c, j = m // 2, m % 2
                    dve.wait_ge(mid_ready, m + 1)
                    dve.wait_ge(rest_ready, m + 1)
                    v.tensor_tensor(chunk(qk_parts[j][:, 2, :], c), qk_rest[:, m % 2, :], chunk(qk_parts[j][:, 1, :], c), ALU.subtract).then_inc(lo_ready, 1)

                for m in range(2 * NC + 2):
                    if m < 2 * NC:
                        rope(m)
                    if 0 <= m - 1 < 2 * NC:
                        rest(m - 1)
                    if 0 <= m - 2:
                        low(m - 2)
                dve.wait_ge(v_pad, 2)
                bv = mat("bv_rows").rearrange("p (h d) -> p h d", h=NH)
                for t in range(TILES):
                    dve.wait_ge(av_ps, TPC * (t // TPC) + TPC)
                    src = psum[:, t // TPC, (t % TPC) * 128:(t % TPC + 1) * 128].rearrange("p (h d) -> p h d", h=NH)
                    v.tensor_tensor(v_all[:, t, :, 0:HD], src, bv, ALU.add).then_inc(v_all_ready, 1)

            def attention():
                dve.sem_inc(s1_read, RING)

                def head(hs, u):
                    for p in range(SN):
                        step, kind, x = STREAM[p]
                        if kind == "row":
                            continue
                        qt, c = x
                        dve.wait_ge(s1_ps, hs * SN + (p + 1))
                        v.tensor_reduce(tile_max[:, qt, c:c + 1], psum[:, 4 + p % RING, :], AX.X, ALU.max).then_inc(s1_read, 1)
                        if qt % 4 == 3 and c == NC - 1:
                            g = qt // 4
                            dve.wait_ge(s1_read, hs * SCORES + ((qt + 1) * NC + RING))
                            v.tensor_reduce(row_max[:, g, :], tile_max[:, 4 * g:4 * g + 4, :], AX.X, ALU.max).then_inc(max_step, 1)
                            dve.wait_ge(max_step, hs * 8 + (2 * g + 1))
                            v.tensor_copy(max_parts[:, g, :, 0], row_max[:, g, :]).then_inc(max_step, 1)
                            dve.wait_ge(max_step, hs * 8 + (2 * g + 2))
                            v.tensor_tensor(max_parts[:, g, :, 1], row_max[:, g, :], max_parts[:, g, :, 0], ALU.subtract).then_inc(max_parts_ready, 1)

                with dve.Fori(0, NH // UN) as i:
                    for u in range(UN):
                        head(i * UN + u, u)
                dve.wait_ge(o_in, 32)
                for k in range(2):
                    dve.wait_ge(o_stored[k], 16 * STORES * (1 + NH // 2))
                v.reciprocal(sums[:], sums[:]).then_inc(inv_ready, 1)
                for c in range(NC):
                    dve.wait_ge(inv_ps, c + 1)
                    v.tensor_tensor(chunk(attnT, c), chunk(attnT, c), psum[:, c, :], ALU.mult).then_inc(attn_ready, 1)

            modulation()
            dve.sem_inc(y_added, 2)
            layer_norm(0, xT, h0T, modc(0, CA), modc(0, SA), ln_in_ready)
            layer_norm(1, h0T, normT, col("ln_g"), col("ln_b"), normed_ready)
            ssm_inputs()
            ssm_scan()
            residual(w2_o_ready, 0)
            layer_norm(2, xT, normT, modc(0, CB), modc(0, SB), normed_ready)
            route(0)
            keep_capacity()
            experts(0)
            layer_norm(3, xT, normT, modc(1, CA), modc(1, SA), normed_ready)
            attention_inputs()
            attention()
            residual(wo_o_ready, 0)
            layer_norm(4, xT, normT, modc(1, CB), modc(1, SB), normed_ready)
            route(1)
            experts(1)


def kernel(**inputs):
    import concourse.bacc as bacc
    from concourse.bass_utils import run_bass_kernel_spmd

    g = {k: np.ascontiguousarray(a) for k, a in inputs.items()}
    ident = np.eye(128, dtype=np.float32)
    quadrant = np.arange(128) // 32
    rotate = np.zeros((128, 128), np.float32)
    rotate[np.arange(1, 128, 2), np.arange(0, 128, 2)] = -1.0
    rotate[np.arange(0, 128, 2), np.arange(1, 128, 2)] = 1.0
    inv_freq = (1.0 / np.float32(THETA) ** (np.arange(0, HD, 2, dtype=np.float32) / np.float32(HD))).astype(np.float32)
    angles = np.tile(np.repeat(np.arange(L, dtype=np.float32)[:, None] * inv_freq[None, :], 2, axis=1), (1, NH)).T
    vectors = {
        "ln_g": g["L0_attn_ln_g"], "ln_b": g["L0_attn_ln_b"], "w1_b": g["L0_attn_w1_b"], "v1_b": g["L0_attn_v1_b"],
        "w2_b": g["L0_attn_w2_b"], "b_dt": g["L0_attn_b_dt"], "D_skip": g["L0_attn_D_skip"],
        "conv0": g["L0_attn_conv_w"][:, 0, 0], "conv1": g["L0_attn_conv_w"][:, 0, 1], "conv2": g["L0_attn_conv_w"][:, 0, 2],
        "c0": g["L0_c"][0], "c1": g["L1_c"][0], "bq": g["L1_attn_bq"], "bk": g["L1_attn_bk"], "bo": g["L1_attn_bo"],
        "part1": np.where(quadrant >= 1, -1.0, 0.0).astype(np.float32),
        "part2": np.where(quadrant >= 2, -1.0, 0.0).astype(np.float32),
    }
    cols = np.concatenate([np.stack([vectors[n] for n in COLS], 1), g["L0_attn_A_log"]], 1)
    bc = np.concatenate([g["L0_attn_W_B"], g["L0_attn_W_C"]], 1)
    matrices = {
        "w1": g["L0_attn_w1_w"], "v1": g["L0_attn_v1_w"], "w2": g["L0_attn_w2_w"], "W_dt": g["L0_attn_W_dt"],
        "W_BC": np.concatenate([bc, bc, bc, np.zeros((128, 32), np.float32)], 1),
        "WqT": g["L1_attn_Wq"].T, "WkT": g["L1_attn_Wk"].T, "WvT": g["L1_attn_Wv"].T, "WoT": g["L1_attn_Wo"].T,
        "ident": ident, "mean": np.full((128, 128), 1.0 / D, np.float32),
        "bv_rows": np.broadcast_to(g["L1_attn_bv"], (128, 128)), "rotate": rotate,
        "group": (np.arange(128)[:, None] // REP == np.arange(128)[None, :] // REP).astype(np.float32),
    }
    mats = np.stack([matrices[n] for n in MATS], 1)
    wmod = np.concatenate([g["L0_wmod"].reshape(128, 6, 128), g["L1_wmod"].reshape(128, 6, 128)], 1)
    p = np.arange(128)[:, None]
    bcsel = ((p % 32 == np.arange(32)[None, :]) & (p < 96)).astype(np.float32)
    spread = ((p[:, :, None] % HD == np.arange(HD)[None, :, None]) & (p[:, :, None] // HD == np.arange(128) // HD)).astype(np.float32)
    shifts = 4 * np.arange(ROUNDS - 1, -1, -1)
    digit = np.minimum(p % REP, np.where(shifts == 28, 4, REP)) << shifts
    router = np.concatenate([
        g["L0_ffn_Wr"], g["L1_ffn_router_w"].T, np.broadcast_to(np.arange(NE, dtype=np.float32) - NE, (128, NE)),
        np.broadcast_to(g["L0_ffn_br"], (128, NE)), np.broadcast_to((2.0 ** shifts).astype(np.float32), (128, ROUNDS))], 1)
    arrays = {"xT_in": g["L0_attn_x"][0].T, "cols_in": cols, "mats_in": mats, "wmod_in": wmod, "bcsel_in": bcsel,
              "router_in": router, "digits_in": digit.astype(np.int32),
              "cos_in": np.cos(angles), "sin_in": np.sin(angles), "zero_in": np.zeros((SHIFT, L // 2), np.float32),
              "spread_in": spread}
    expert_arrays = [
        {"w1_0": g["L0_ffn_W1"], "w2_0": g["L0_ffn_W2"].reshape(NE, HC, 128, D).transpose(0, 2, 1, 3),
         "b1_0": g["L0_ffn_b1"].reshape(NE, HC, 128).transpose(0, 2, 1), "b2_0": g["L0_ffn_b2"][:, :, None]},
        {"w1_1": g["L1_ffn_w1"], "w2_1": g["L1_ffn_w2"].reshape(NE, HC, 128, D).transpose(0, 2, 1, 3)},
    ]
    arrays.update(expert_arrays[0])
    arrays.update(expert_arrays[1])
    arrays = {k: np.ascontiguousarray(a) for k, a in arrays.items()}

    nc = bacc.Bacc("TRN2", target_bir_lowering=False, num_devices=1)
    ins = {k: nc.dram_tensor(k, a.shape, mybir.dt.from_np(a.dtype), kind="ExternalInput").ap() for k, a in arrays.items()}
    moe_in = [[ins.pop(n) for n in e] for e in expert_arrays]
    out = nc.dram_tensor("outT", (128, L), F32, kind="ExternalOutput").ap()
    build(nc, *ins.values(), moe_in, out)
    r = run_bass_kernel_spmd(nc, [arrays], core_ids=[0])
    return np.ascontiguousarray(r.results[0]["outT"].T)[None]
```

```python
from contextlib import ExitStack

import numpy as np

import concourse.bass as bass
from concourse import mybir

F32 = mybir.dt.float32
BF16 = mybir.dt.bfloat16
ALU = mybir.AluOpType
ACT = mybir.ActivationFunctionType
AX = mybir.AxisListType

D = 128
L = 2048
C = 512
NC = L // C
TILES = L // 128
TPC = C // 128
HALF = L // 2
NS = 16
UNS = 4
EPS = 1e-5

COLS = ["ln_g", "ln_b", "w1_b", "v1_b", "w2_b", "b_dt", "D_skip", "conv0", "conv1", "conv2",
        "c0", "c1", "bq", "bk", "bo", "part1", "part2"]
COL = {n: i for i, n in enumerate(COLS)}
A_LOG = len(COLS)
NCOLS = A_LOG + NS
MATS = ["mean", "ident", "w1", "v1", "w2", "W_dt", "W_BC", "WqT", "WkT", "WvT", "WoT", "group", "rotate", "bv_rows"]
FIRST_MATS = 4
MAT = {n: i for i, n in enumerate(MATS)}
SA, CA, GA, SB, CB, GB = range(6)

NE = 8
HC = 4
CAP = 308
REP = 128 // NE
EARLY = 2
ROUND_MMS = 5
ROUNDS = 8
I32 = mybir.dt.int32


NH = 16
HD = D // NH
UN = 4
KT = TILES
SCALE = float(HD) ** -0.5
THETA = 10000.0
TWO_MINUS_ONES = float(np.array([0xBF80BF80], np.uint32).view(np.float32)[0])
SHIFT = 2
GROUP = 3 * HD
VM = 32
SPAN = L // HD
STORES = NC + 1
STACK_LOADS = 5


def maxima_stream():
    found = []
    for step in range(KT):
        found += [(step, "scores", (step, c)) for c in range(NC)]
        if step and step % 4 == 0:
            found.append((step, "row", step // 4 - 1))
    found.append((KT, "row", KT // 4 - 1))
    return found


STREAM = maxima_stream()
SN = len(STREAM)
RING = 3
assert SN % RING == 2
SCORES = KT * NC
ROWS = KT // 4
AHEAD = 2


def build(nc, xT_in, cols_in, mats_in, wmod_in, bcsel_in, router_in, digits_in, cos_in, sin_in, zero_in, spread_in, moe_in, out):
    with ExitStack() as ctx:
        def sb(name, shape, dt=F32):
            return ctx.enter_context(nc.sbuf_tensor(name, shape, dt))

        def phase():
            inner = ExitStack()
            return inner, lambda name, shape, dt=F32: inner.enter_context(nc.sbuf_tensor(name, shape, dt))

        def sem(name):
            return ctx.enter_context(nc.semaphore(name))

        psum = ctx.enter_context(nc.psum_tensor("psum", [128, 8, C], F32))

        def banks(b, n):
            return psum[:, b:b + n, :].rearrange("p b c -> p (b c)")

        cols = sb("cols", [128, NCOLS])
        mats = sb("mats", [128, len(MATS), 128])
        wmod = sb("wmod", [128, 12, 128])
        bcsel_f = sb("bcsel_f", [128, 2 * NS])
        bcsel = sb("bcsel", [128, 2 * NS], BF16)
        silu_c = sb("silu_c", [128, 2])
        mod = sb("mod", [128, 12])
        gate_sign = sb("gate_sign", [128, 4])
        gate_size = sb("gate_size", [128, 4])
        gated_w2b = sb("gated_w2b", [128, 1])
        diag_skip = sb("diag_skip", [128, 128])
        eps_col = sb("eps_col", [128, 1])

        xT = sb("xT", [128, L])
        h0T = sb("h0T", [128, L])
        normT = sb("normT", [128, L])
        ln_xc = sb("ln_xc", [128, L])
        ln_sq = sb("ln_sq", [128, 2, C])
        ln_std = sb("ln_std", [128, 2, TPC])
        ln_rstd = sb("ln_rstd", [128, 2, TPC])
        ln_xn = sb("ln_xn", [128, 2, C])

        def col(name):
            return cols[:, COL[name]:COL[name] + 1]

        def mat(name):
            return mats[:, MAT[name], :]

        def modc(layer, j):
            return mod[:, 6 * layer + j:6 * layer + j + 1]

        proj_o = sb("proj_o", [128, 2, C])
        router = sb("router", [128, 2 * NE + 2 * NE + ROUNDS])
        router_w = [router[:, 0:NE], router[:, NE:2 * NE]]
        expert_no = router[:, 2 * NE:3 * NE]
        router_b = router[:, 3 * NE:4 * NE]
        digit_size = router[:, 4 * NE:4 * NE + ROUNDS]
        digits = sb("digits", [128, ROUNDS], I32)
        rt = {n: sb(f"rt_{n}", [128, TILES, NE]) for n in ["logit", "prob", "eq", "best1", "rest", "best2", "gate"]}
        rs = {n: sb(f"rs_{n}", [128, TILES]) for n in ["max", "sum", "inv", "top1", "no", "top2"]}
        gate_wide = ln_xc[:].rearrange("p (t e r) -> p t e r", t=TILES, e=NE)
        gates_rep = h0T
        thr = {n: sb(f"thr_{n}", [128, 1], I32) for n in ["low", "try", "add"]}
        thr_f = {n: sb(f"thr_{n}", [128, 1]) for n in ["count", "keep", "quota"]}
        w1s = sb("w1s", [128, 2, HC * 128])
        w2s = sb("w2s", [128, 2, HC, 128])
        b1s = sb("b1s", [128, 2, HC])
        b2s = sb("b2s", [128, 2, 1])
        gates_dram = [nc.dram_tensor(f"gates_dram{n}", (NE, L), F32).ap() for n in range(2)]

        ident_b = sb("ident_b", [128, 128], BF16)
        tile_max = sb("tile_max", [128, KT, NC])
        row_max = sb("row_max", [128, 4, 4])
        max_parts = sb("max_parts", [128, 4, 4, SHIFT], BF16)
        gated_bo = sb("gated_bo", [128, 1])
        o_sb = sb("o_sb", [128, 2, C])
        sums = sb("sums", [128, SPAN])
        spread_sums = sb("spread_sums", [128, HD, 128])

        ssm_scope, ssm_sb = phase()
        x1pad = ssm_sb("x1pad", [128, L + 2])
        conv_a = ssm_sb("conv_a", [128, 2, C])
        conv_b = ssm_sb("conv_b", [128, 2, C])
        vT = ssm_sb("vT", [128, L])
        uT = ssm_sb("uT", [128, L])
        dt_x = ssm_sb("dt_x", [128, L])
        dt_z = ssm_sb("dt_z", [128, L])
        dt_w = ssm_sb("dt_w", [128, L])
        dt_ln = ssm_sb("dt_ln", [128, L])
        conv_y, bc_r1, dt_abs, dt_e, dt_r = h0T, normT, dt_z, dt_z, dt_ln
        dtT = ssm_sb("dtT", [128, L])
        dtuT = ssm_sb("dtuT", [128, L])
        bc_p1 = ssm_sb("bc_p1", [128, L], BF16)
        bc_p2 = ssm_sb("bc_p2", [128, L], BF16)
        bc_parts = ssm_sb("bc_parts", [128, L], BF16)
        expA = ssm_sb("expA", [128, NS])
        negA = ssm_sb("negA", [128, NS])
        ssm_dA = ssm_sb("ssm_dA", [128, 2, HALF])
        ssm_b = dt_z[:].rearrange("p (k t) -> p k t", k=2)
        ssm_dBu = dt_ln[:].rearrange("p (k t) -> p k t", k=2)
        ssm_h = ssm_sb("ssm_h", [128, 2, HALF])
        ssm_g = ssm_sb("ssm_g", [128, 2, HALF])
        ssm_carry = ssm_sb("ssm_carry", [128, NS])
        yvT = dt_x
        ssm_scope.close()

        moe_scope, moe_sb = phase()
        gate_eq = moe_sb("gate_eq", [128, L])
        gate_rank = moe_sb("gate_rank", [128, L])
        gate_valid = moe_sb("gate_valid", [128, L])
        gate_bc = moe_sb("gate_bc", [128, 2, L])
        hidden = moe_sb("hidden", [128, 2, HC, C])
        gated = moe_sb("gated", [128, 2, C])
        moe_acc = moe_sb("moe_acc", [128, L])
        early_out = moe_sb("early_out", [128, EARLY, L])
        moe_scope.close()

        attn_scope, attn_sb = phase()
        qkT = [attn_sb(n, [128, L]) for n in ("qT", "kT")]
        cosT = attn_sb("cosT", [128, L])
        sinT = attn_sb("sinT", [128, L])
        attn_scope.close()
        attn_scope, attn_sb = phase()
        probs = attn_sb("probs", [128, 4, L])
        qk_parts = [attn_sb(n, [128, 3, L], BF16) for n in ("q_parts", "k_parts")]
        rope_cos = attn_sb("rope_cos", [128, 2, C])
        rope_sin = attn_sb("rope_sin", [128, 2, C])
        qk_rest = attn_sb("qk_rest", [128, 2, C])
        q_stack = attn_sb("q_stack", [128, UN, L], BF16)
        k_stack = attn_sb("k_stack", [128, UN, L], BF16)
        v_all = attn_sb("v_all", [128, KT, NH, HD + 1])
        v_head = attn_sb("v_head", [128, UN, KT, VM])
        attn_scope.close()
        attnT = h0T
        parts_dram = [nc.dram_tensor(n, (128, 3, L), BF16).ap() for n in ("q_dram", "k_dram")]
        o_dram = nc.dram_tensor("o_dram", (128, NC, C), F32).ap()
        sums_dram = nc.dram_tensor("sums_dram", (NH, NC, C), F32).ap()

        params_in = sem("params_in")
        mats_loaded = sem("mats_loaded")
        x_in = [sem(f"x_in{c}") for c in range(NC)]
        wmod_loaded = sem("wmod_loaded")
        router_loaded = sem("router_loaded")
        out_done = sem("out_done")
        silu_c_ready = sem("silu_c_ready")
        mod_ps_ready = sem("mod_ps_ready")
        mod_step = sem("mod_step")
        mod_ready = sem("mod_ready")
        constants_ready = sem("constants_ready")
        bcsel_ready = sem("bcsel_ready")
        diag_ready = sem("diag_ready")
        ln_in_ready = sem("ln_in_ready")
        ln_mean_ready = sem("ln_mean_ready")
        ln_xc_ready = sem("ln_xc_ready")
        ln_sq_ready = sem("ln_sq_ready")
        ln_var_ready = sem("ln_var_ready")
        ln_std_ready = sem("ln_std_ready")
        ln_rstd_ready = sem("ln_rstd_ready")
        ln_xn_ready = sem("ln_xn_ready")
        ln_bc_ready = sem("ln_bc_ready")
        normed_ready = sem("normed_ready")
        x1_ps = sem("x1_ps")
        v_ps = sem("v_ps")
        x1_ready = sem("x1_ready")
        v_ready = sem("v_ready")
        pad_ready = sem("pad_ready")
        conv_step = sem("conv_step")
        conv_ready = sem("conv_ready")
        u_ready = sem("u_ready")
        dt_ps = sem("dt_ps")
        bc_ps = sem("bc_ps")
        dt_x_ready = sem("dt_x_ready")
        bc_p1_ready = sem("bc_p1_ready")
        bc_r1_ready = sem("bc_r1_ready")
        bc_p2_ready = sem("bc_p2_ready")
        bc_parts_ready = sem("bc_parts_ready")
        dt_abs_ready = sem("dt_abs_ready")
        dt_z_ready = sem("dt_z_ready")
        dt_w_ready = sem("dt_w_ready")
        dt_ln_ready = sem("dt_ln_ready")
        dt_e_ready = sem("dt_e_ready")
        dt_r_ready = sem("dt_r_ready")
        dt_ready = sem("dt_ready")
        dtu_ready = sem("dtu_ready")
        expA_ready = sem("expA_ready")
        negA_ready = sem("negA_ready")
        b_bc_ready = sem("b_bc_ready")
        c_bc_ready = sem("c_bc_ready")
        b_copied = sem("b_copied")
        dBu_ready = sem("dBu_ready")
        g_ready = sem("g_ready")
        dA_ready = sem("dA_ready")
        scan_done = sem("scan_done")
        carry_done = sem("carry_done")
        y_added = sem("y_added")
        yv_ready = sem("yv_ready")
        w2_ps = sem("w2_ps")
        w2_o_ready = sem("w2_o_ready")

        thr_count_done = sem("thr_count_done")
        early_copied, early_gated = sem("early_copied"), sem("early_gated")
        qk_ps, qk_raw, rot_ps = sem("qk_ps"), sem("qk_raw"), sem("rot_ps")
        tables_in = sem("tables_in")
        cos_ready, sin_ready, roped = sem("cos_ready"), sem("sin_ready"), sem("roped")
        hi_ready, rest_ready, mid_ready, lo_ready = (sem(n) for n in ("hi_ready", "rest_ready", "mid_ready", "lo_ready"))
        parts_stored = sem("parts_stored")
        stack_step, stacks_clear = sem("stack_step"), sem("stacks_clear")
        stack_in = [sem(f"stack_in{u}") for u in range(UN)]
        av_ps, v_pad, v_all_ready, v_head_ready = sem("av_ps"), sem("v_pad"), sem("v_all_ready"), sem("v_head_ready")
        s1_ps, s1_read, row_copied, max_step, max_parts_ready = (sem(n) for n in ("s1_ps", "s1_read", "row_copied", "max_step", "max_parts_ready"))
        s2_ps, p_ready, pv_done, o_copied = (sem(n) for n in ("s2_ps", "p_ready", "pv_done", "o_copied"))
        o_stored = [sem(f"o_stored{k}") for k in range(2)]
        o_in, inv_ready, inv_ps = (sem(n) for n in ("o_in", "inv_ready", "inv_ps"))
        attn_ready, wo_ps, wo_o_ready = sem("attn_ready"), sem("wo_ps"), sem("wo_o_ready")
        names = ["logits_ready", "route_step", "exp_ready", "wide_ready", "rep_ps", "rep_ready", "thr_step",
                 "thr_counted", "gates_final", "gates_stored", "hid_ps", "hid_ready", "out_ps", "out_gated", "acc_done"]
        ms = []
        for layer in range(2):
            m = {n: sem(f"l{layer}_{n}") for n in names}
            m["weights_in"] = [sem(f"l{layer}_weights_in{k}") for k in range(2)]
            m["gates_in"] = [sem(f"l{layer}_gates_in{k}") for k in range(2)]
            ms.append(m)

        block = ctx.enter_context(nc.Block())

        def ln_steps(first, count, *parts):
            for s in range(NC * first, NC * (first + count) + 3):
                for part, behind in parts:
                    if NC * first <= s - behind < NC * (first + count):
                        part(s - behind)

        def c_bank(hf, k):
            return 2 if k == 0 else (6, 4)[hf]

        def chunk(t, c):
            return t[:, c * C:(c + 1) * C]

        def half(t, hf):
            return t[:, hf * HALF:(hf + 1) * HALF]

        @block.sync
        def _(sp):
            sp.dma_start(cols[:], cols_in).then_inc(params_in, 16)
            sp.dma_start(mats[:, :FIRST_MATS], mats_in[:, :FIRST_MATS]).then_inc(params_in, 16)
            sp.dma_start(bcsel_f[:], bcsel_in).then_inc(params_in, 16)
            for c in range(NC):
                sp.dma_start(chunk(xT, c), chunk(xT_in, c)).then_inc(x_in[c], 16)
            sp.dma_start(mats[:, FIRST_MATS:], mats_in[:, FIRST_MATS:]).then_inc(mats_loaded, 16)
            sp.dma_start(router[:], router_in).then_inc(router_loaded, 16)
            sp.dma_start(digits[:], digits_in).then_inc(router_loaded, 16)

            def moe(layer):
                m = ms[layer]
                w1_in, w2_in = moe_in[layer][:2]

                def weights(e, k):
                    at = bass.ds(e, 1)
                    sp.dma_start(w1s[:, k, :], w1_in[at].rearrange("o p f -> (o p) f")).then_inc(m["weights_in"][k], 16)
                    sp.dma_start(w2s[:, k, :, :], w2_in[at].rearrange("o p c d -> (o p) c d")).then_inc(m["weights_in"][k], 16)
                    if layer == 0:
                        b1_in, b2_in = moe_in[layer][2:]
                        sp.dma_start(b1s[:, k, :], b1_in[at].rearrange("o p c -> (o p) c")).then_inc(m["weights_in"][k], 16)
                        sp.dma_start(b2s[:, k, :], b2_in[at].rearrange("o p c -> (o p) c")).then_inc(m["weights_in"][k], 16)

                def gates(e, k):
                    sp.dma_start(gate_bc[:, k, :], gates_dram[layer][bass.ds(e, 1)].rearrange("o t -> (o t)").partition_broadcast(128)).then_inc(m["gates_in"][k], 16)

                if layer:
                    sp.wait_ge(ms[0]["out_gated"], 2 + NE * NC)
                for k in range(2):
                    weights(k, k)
                if layer == 0:
                    sp.wait_ge(early_copied, NC)
                    weights(EARLY, 0)
                sp.wait_ge(m["rep_ready"] if layer else m["gates_final"], 1)
                final = gates_rep if layer else gate_valid
                sp.dma_start(gates_dram[layer], final[0:128:REP, :]).then_inc(m["gates_stored"], 16)
                sp.wait_ge(m["gates_stored"], 16)
                for k in range(2):
                    gates(k, k)
                if layer == 0:
                    sp.wait_ge(early_copied, 2 * NC)
                    weights(EARLY + 1, 1)
                    for k in range(EARLY):
                        sp.wait_ge(early_gated, NC * (k + 1))
                        gates(EARLY + k, k)
                with sp.Fori(1 if layer else 2, NE // 2) as i:
                    for k in range(2):
                        sp.wait_ge(m["out_gated"], i * 2 * NC + (NC * (k - 1) + 2))
                        weights(i * 2 + k, k)
                        gates(i * 2 + k, k)

            def attention():
                sp.wait_ge(ln_in_ready, 3 * NC)
                sp.dma_start(cosT[:], cos_in).then_inc(tables_in, 16)
                sp.dma_start(sinT[:], sin_in).then_inc(tables_in, 16)
                sp.dma_start(spread_sums[:], spread_in).then_inc(tables_in, 16)
                for hf in range(2):
                    sp.wait_ge(lo_ready, 4 * hf + 4)
                    sp.wait_ge(mid_ready, 4 * hf + 4)
                    for j in range(2):
                        at = slice(hf * HALF, (hf + 1) * HALF)
                        sp.dma_start(parts_dram[j][:, :, at], qk_parts[j][:, :, at]).then_inc(parts_stored, 16)
                sp.wait_ge(parts_stored, 64)
                sp.wait_ge(stacks_clear, 1)

                def stack(h, u):
                    rows = bass.ds(h * HD, HD)
                    q, k = q_stack[:, u, :], k_stack[:, u, :]
                    sp.dma_start(q[0:SHIFT].bitcast(F32), zero_in).then_inc(stack_in[u], 16)
                    q_rows = parts_dram[0][rows].rearrange("i b t -> (i b) t").unsqueeze(0).to_broadcast([3, GROUP, L])
                    sp.dma_start(q[SHIFT:SHIFT + 3 * GROUP], q_rows).then_inc(stack_in[u], 16)
                    for a in range(3):
                        lo = SHIFT + a * GROUP
                        k_rows = parts_dram[1][rows, a, :].unsqueeze(1).to_broadcast([HD, 3, L])
                        sp.dma_start(k[lo:lo + GROUP], k_rows).then_inc(stack_in[u], 16)

                def store(u, sums_at, o_at):
                    sp.dma_start(sums_at, o_sb[HD:128:32, u % 2, :]).then_inc(o_stored[u % 2], 16)
                    for j in range(NC):
                        sp.dma_start(o_at(j), o_sb[32 * j:32 * j + HD, u % 2, :]).then_inc(o_stored[u % 2], 16)

                for u in range(UN):
                    stack(u, u)
                with sp.Fori(0, NH // UN - 1) as i:
                    for u in range(UN):
                        h = i * UN + u
                        sp.wait_ge(o_copied, h + 2)
                        store(u, sums_dram[bass.ds(h, 1)].rearrange("o j t -> (o j) t"), lambda j: o_dram[bass.ds(h * HD, HD), j, :])
                        sp.wait_ge(s2_ps, h * 2 * KT + 2 * KT)
                        stack(h + UN, u)
                for u in range(UN):
                    h = NH - UN + u
                    sp.wait_ge(o_copied, h + 2)
                    if u == 0:
                        for k in range(2):
                            sp.wait_ge(o_stored[k], 16 * STORES * (1 + h // 2))
                        sp.dma_start(sums[0:h * HD, :], sums_dram[0:h].rearrange("h j t -> (h j t)").rearrange("(p t) -> p t", t=SPAN)).then_inc(o_in, 16)
                        sp.dma_start(attnT[0:h * HD, :], o_dram[0:h * HD].rearrange("r j t -> r (j t)")).then_inc(o_in, 16)
                    at = slice(h * HD, (h + 1) * HD)
                    store(u, sums[at, :], lambda j: attnT[at, j * C:(j + 1) * C])

            moe(0)
            attention()
            moe(1)
            for c in range(NC):
                sp.wait_ge(ln_in_ready, 4 * NC + c + 1)
                sp.dma_start(chunk(out, c), chunk(xT, c)).then_inc(out_done, 16)
            sp.wait_ge(out_done, 16 * NC)

        @block.tensor
        def _(pe):
            mm = nc.tensor.matmul

            def modulation():
                pe.wait_ge(wmod_loaded, 16)
                pe.wait_ge(silu_c_ready, 1)
                for j in range(12):
                    i = mm(psum[:, 7, j:j + 1], wmod[:, j, :], silu_c[:, j // 6:j // 6 + 1],
                           start=True, stop=True)
                i.then_inc(mod_ps_ready, 1)

            def layer_norms(first, *sources):
                def mean(n):
                    k, c = n // NC, n % NC
                    if k == 0:
                        pe.wait_ge(x_in[c], 16)
                    else:
                        pe.wait_ge(ln_in_ready, n - NC + 1)
                    if k > first:
                        pe.wait_ge(ln_xc_ready, n - NC + 1)
                    mm(psum[:, c, :], mat("mean"), chunk(sources[k - first], c), start=True, stop=True).then_inc(ln_mean_ready, 1)
                    if n == 1:
                        modulation()

                def var(n):
                    c = n % NC
                    pe.wait_ge(ln_sq_ready, n + 1)
                    if n // NC > first:
                        pe.wait_ge(ln_xn_ready, n - NC + 1)
                    for t in range(TPC):
                        i = mm(psum[:, 4 + c, t:t + 1], ln_sq[:, c % 2, t * 128:(t + 1) * 128], mat("mean")[:, 0:1],
                               start=True, stop=True)
                    i.then_inc(ln_var_ready, 1)

                def spread_rstd(n):
                    c = n % NC
                    pe.wait_ge(ln_rstd_ready, n + 1)
                    for t in range(TPC):
                        i = mm(psum[:, 4 + c, t * 128:(t + 1) * 128],
                               ln_rstd[:, c % 2, t:t + 1].to_broadcast([128, 128]), mat("ident"), start=True, stop=True)
                    i.then_inc(ln_bc_ready, 1)

                ln_steps(first, len(sources), (var, 2), (spread_rstd, 3), (mean, 0))

            def ssm_inputs():
                for c in range(NC):
                    pe.wait_ge(normed_ready, c + 1)
                    mm(psum[:, c, :], mat("w1"), chunk(normT, c), start=True, stop=True).then_inc(x1_ps, 1)
                    mm(psum[:, 4 + c, :], mat("v1"), chunk(normT, c), start=True, stop=True).then_inc(v_ps, 1)
                pe.wait_ge(mats_loaded, 16)
                for c in range(NC):
                    pe.wait_ge(x1_ready, c + 1)
                    pe.wait_ge(v_ready, c + 1)
                    pe.wait_ge(u_ready, c + 1)
                    mm(psum[:, c, :], mat("W_dt"), chunk(uT, c), start=True, stop=True).then_inc(dt_ps, 1)
                    mm(psum[:, 4 + c, :], mat("W_BC"), chunk(uT, c), start=True, stop=True).then_inc(bc_ps, 1)

            def ssm_scan():
                def spread(bank, hf, column, done):
                    for j in range(2):
                        at = hf * HALF + j * C
                        i = mm(psum[:, bank + j, :], bcsel[:, bass.ds(column, 1)].to_broadcast([128, 128]),
                               bc_parts[:, at:at + C], start=True, stop=True)
                    i.then_inc(done, 1)

                def spread_b(hf, n, column):
                    pe.wait_ge(b_copied, n)
                    spread(0, hf, column, b_bc_ready)

                def spread_c(hf, n, k, column):
                    pe.wait_ge(g_ready, n + 1)
                    spread(c_bank(hf, k), hf, column + NS, c_bc_ready)

                def add_y(hf, n, slot, last):
                    pe.wait_ge(g_ready, n + 3)
                    for j in range(2):
                        i = mm(psum[:, 4 + 2 * hf + j, :], mat("ident"), ssm_g[:, slot, j * C:(j + 1) * C],
                               start=False, stop=last, skip_group_check=True)
                    i.then_inc(y_added, 1)

                def state(hf, i, k, first=False, last=False):
                    n = i * UNS + (hf * NS + k)
                    column = i * UNS + k
                    spread_c(hf, n, k % 2, column)
                    if not last or k < UNS - 2:
                        spread_b(hf, n + 2, column + 2)
                    elif hf == 0:
                        spread_b(1, n + 2, k + 2 - UNS)
                    if not first:
                        add_y(hf, n - 1, (k + 1) % 2, False)
                    if last and k == UNS - 1:
                        add_y(hf, n, k % 2, True)

                pe.wait_ge(bc_parts_ready, 2)
                pe.wait_ge(dt_x_ready, 2)
                pe.wait_ge(dt_abs_ready, 2)
                pe.wait_ge(bcsel_ready, 1)
                pe.wait_ge(diag_ready, 1)
                spread(0, 0, 0, b_bc_ready)
                spread_b(0, 1, 1)
                for hf in range(2):
                    for j in range(2):
                        mm(psum[:, 4 + 2 * hf + j, :], diag_skip[:], chunk(uT, 2 * hf + j),
                           start=True, stop=False, skip_group_check=True)
                    for k in range(UNS):
                        if hf and k == 1:
                            pe.wait_ge(yv_ready, 1)
                        state(hf, 0, k, first=k == 0)
                    with pe.Fori(1, NS // UNS - 1) as i:
                        for k in range(UNS):
                            state(hf, i, k)
                    for k in range(UNS):
                        state(hf, NS // UNS - 1, k, last=True)

            def ssm_out():
                for c in range(NC):
                    pe.wait_ge(yv_ready, c // 2 + 1)
                    if c == 0:
                        pe.wait_ge(g_ready, 2 * NS + 2)
                    mm(psum[:, c, :], mat("w2"), chunk(yvT, c), start=True, stop=True).then_inc(w2_ps, 1)

            def route(layer, done):
                m = ms[layer]
                pe.wait_ge(router_loaded, 32)
                for t in range(TILES):
                    if t % TPC == 0:
                        pe.wait_ge(normed_ready, done + t // TPC + 1)
                    i = mm(psum[:, 4, t * NE:(t + 1) * NE], normT[:, t * 128:(t + 1) * 128], router_w[layer],
                           start=True, stop=True)
                i.then_inc(m["logits_ready"], 1)

            def spread_gates(layer):
                m = ms[layer]
                pe.wait_ge(m["wide_ready"], 1)
                for t in range(TILES):
                    i = mm(psum[:, 4 + t // TPC, (t % TPC) * 128:(t % TPC + 1) * 128],
                           ln_xc[:, t * 128:(t + 1) * 128], mat("ident"), start=True, stop=True)
                i.then_inc(m["rep_ps"], 1)

            def experts(layer):
                m = ms[layer]
                pe.sem_inc(m["out_ps"], 2)
                done = {"mms": 0, "rounds": ROUNDS}

                def between():
                    done["mms"] += 1
                    if done["mms"] % ROUND_MMS == 0 and done["rounds"] < ROUNDS:
                        pe.wait_ge(m["thr_step"], done["rounds"] * 6 + 3)
                        mm(psum[:, 6, 0:1], mat("group"), thr_f["keep"][:], start=True, stop=True).then_inc(m["thr_counted"], 1)
                        done["rounds"] += 1

                def up(i, k, tb):
                    n = i * 2 * NC + (k * NC + tb)
                    if tb == 0:
                        pe.wait_ge(m["weights_in"][k], (i + 1) * (64 if layer == 0 else 32))
                    for hc in range(HC):
                        between()
                        pe.wait_ge(m["hid_ready"], n * HC + (hc + 1))
                        mm(psum[:, hc, :], w1s[:, k, hc * 128:(hc + 1) * 128], chunk(normT, tb),
                           start=True, stop=True).then_inc(m["hid_ps"], 1)

                def down(i, k, tb):
                    n = i * 2 * NC + (k * NC + tb)
                    pe.wait_ge(m["hid_ready"], n * HC + 2 * HC)
                    if isinstance(n, int) and layer == 0 and n < EARLY * NC:
                        if n >= 2:
                            pe.wait_ge(early_copied, n - 1)
                    else:
                        pe.wait_ge(m["out_gated"], n + 1)
                    for hc in range(HC):
                        between()
                        j = mm(psum[:, 4 + tb % 2, :], w2s[:, k, hc, :], hidden[:, tb % 2, hc, :],
                               start=hc == 0, stop=hc == HC - 1)
                    j.then_inc(m["out_ps"], 1)

                def pair(i, first=False, last=False):
                    for q in range(2 * NC):
                        if first and q == 0:
                            pass
                        elif q + 1 < 2 * NC:
                            up(i, (q + 1) // NC, (q + 1) % NC)
                        elif not last:
                            up(i + 1, 0, 0)
                        down(i, q // NC, q % NC)

                up(0, 0, 0)
                up(0, 0, 1)
                spread_gates(layer)
                pe.wait_ge(m["rep_ready"], 1)
                if layer == 0:
                    done.update(mms=0, rounds=0)
                pair(0, first=True)
                if layer == 0:
                    pe.wait_ge(early_copied, EARLY * NC)
                with pe.Fori(1, NE // 2 - 1) as i:
                    pair(i)
                pair(NE // 2 - 1, last=True)

            def attention_inputs():
                done = 2 * NC
                pe.wait_ge(ln_xn_ready, 4 * NC)

                def project(m):
                    c, j = m // 2, m % 2
                    pe.wait_ge(normed_ready, done + c + 1)
                    if m >= 2:
                        pe.wait_ge(qk_raw, m - 1)
                    mm(psum[:, 4 + j, :], mat(("WqT", "WkT")[j]), chunk(normT, c), start=True, stop=True).then_inc(qk_ps, 1)

                def rotate(m):
                    c, j = m // 2, m % 2
                    pe.wait_ge(qk_raw, m + 1)
                    if m >= 2:
                        pe.wait_ge(sin_ready, m - 1)
                    mm(psum[:, 6 + j, :], mat("rotate"), chunk(qkT[j], c), start=True, stop=True).then_inc(rot_ps, 1)

                project(0)
                for m in range(2 * NC):
                    if m + 1 < 2 * NC:
                        project(m + 1)
                    rotate(m)
                for t in range(TILES):
                    mm(psum[:, t // TPC, (t % TPC) * 128:(t % TPC + 1) * 128], normT[:, t * 128:(t + 1) * 128], mat("WvT"),
                       start=True, stop=True).then_inc(av_ps, 1)

            def attention():
                pe.wait_ge(constants_ready, 2)
                pe.wait_ge(v_all_ready, TILES)
                pe.wait_ge(sin_ready, 2 * NC)
                pe.sem_inc(pv_done, 4)

                def ring(hs, p):
                    before, heads_back = (p - RING, 0) if p >= RING else ((SN - 2, SN - 1, SN - 3)[p], 1)
                    _, kind, x = STREAM[before]
                    if kind == "row":
                        pe.wait_ge(row_copied, hs * ROWS + (x + 1 + ROWS * (1 - heads_back)))
                    else:
                        qt, c = x
                        pe.wait_ge(s1_read, hs * SCORES + (qt * NC + c + 1 + RING - SCORES * heads_back))
                    return psum[:, 4 + p % RING, :]

                def maxima(hs, u, p, turn=0):
                    step, kind, x = STREAM[p]
                    if p == 0:
                        pe.wait_ge(stack_in[u], turn * (16 * STACK_LOADS) + 16 * STACK_LOADS)
                    bank = ring(hs, p)
                    if kind == "scores":
                        qt, c = x
                        i = mm(bank, q_stack[:, u, qt * 128:(qt + 1) * 128], k_stack[:, u, c * C:(c + 1) * C], start=True, stop=True)
                    else:
                        pe.wait_ge(max_parts_ready, hs * 4 + (x + 1))
                        for j in range(4):
                            i = mm(bank[0:SHIFT, j * 128:(j + 1) * 128], max_parts[:, x, j, :], ident_b[:], start=True, stop=True)
                    i.then_inc(s1_ps, 1)

                def scores(h, u, t):
                    if t == 0:
                        pe.wait_ge(row_copied, h * ROWS + 2 * ROWS)
                    pe.wait_ge(p_ready, h * 2 * KT + (t + 1))
                    kt, b = t // 2, t % 2
                    for j in range(2):
                        at = b * HALF + j * C
                        i = mm(psum[:, 2 * b + j, :], k_stack[:, u, kt * 128:(kt + 1) * 128], q_stack[:, u, at:at + C], start=True, stop=True)
                    i.then_inc(s2_ps, 1)

                def values(h, u, kt):
                    if kt == 0:
                        pe.wait_ge(v_head_ready, h + 1)
                        pe.wait_ge(o_copied, h + 1)
                    pe.wait_ge(p_ready, h * 2 * KT + (2 * kt + 4))
                    for j in range(NC):
                        i = mm(psum[32 * j:32 * j + VM, 7, :], v_head[:, u, kt, :], probs[:, kt % 4, j * C:(j + 1) * C],
                               start=kt == 0, stop=kt == KT - 1)
                    i.then_inc(pv_done, 1)

                def head(h, u, turn, following=NH):
                    for kt in range(KT):
                        s = kt + AHEAD
                        mine = [(1, p) for p in range(SN) if STREAM[p][0] == s]
                        if s >= KT:
                            mine += [(2, p) for p in range(SN) if STREAM[p][0] == s - KT]
                        mine = [(d, p) for d, p in mine if d <= following]

                        def take(n):
                            for d, p in mine[:n]:
                                maxima(h + d, (u + d) % UN, p, turn + (u + d) // UN)
                            del mine[:n]

                        late = s == KT
                        scores(h, u, 2 * kt)
                        take(0 if late else 1)
                        scores(h, u, 2 * kt + 1)
                        take(0 if late else 1)
                        if kt:
                            values(h, u, kt - 1)
                        take(len(mine))
                    values(h, u, KT - 1)

                for p in range(SN):
                    maxima(0, 0, p)
                for p in range(SN):
                    if STREAM[p][0] < AHEAD:
                        maxima(1, 1, p)
                with pe.Fori(0, NH // UN - 1) as i:
                    for u in range(UN):
                        head(i * UN + u, u, i)
                for u in range(UN):
                    head(NH - UN + u, u, NH // UN - 1, following=UN - 1 - u)

            def attention_out():
                pe.wait_ge(inv_ready, 1)
                pe.wait_ge(p_ready, 2 + 2 * KT * NH)
                for i in range(HD):
                    j = mm(banks(0, 4)[:, i * SPAN:(i + 1) * SPAN], spread_sums[:, i, :], sums[:], start=True, stop=True)
                    if (i + 1) * SPAN % C == 0:
                        j.then_inc(inv_ps, 1)
                pe.wait_ge(o_copied, 1 + NH)
                for c in range(NC):
                    pe.wait_ge(attn_ready, c + 1)
                    mm(psum[:, 4 + c, :], mat("WoT"), chunk(attnT, c), start=True, stop=True).then_inc(wo_ps, 1)

            pe.wait_ge(params_in, 48)
            layer_norms(0, xT, h0T)
            ssm_inputs()
            ssm_scan()
            ssm_out()
            layer_norms(2, xT)
            route(0, NC)
            experts(0)
            layer_norms(3, xT)
            attention_inputs()
            attention()
            attention_out()
            layer_norms(4, xT)
            route(1, 3 * NC)
            experts(1)

        @block.scalar
        def _(act):
            f = nc.scalar.activation

            def modulation():
                act.dma_start(wmod[:], wmod_in).then_inc(wmod_loaded, 16)
                act.wait_ge(params_in, 48)
                f(silu_c[:], cols[:, COL["c0"]:COL["c0"] + 2], ACT.Silu).then_inc(silu_c_ready, 1)

            def layer_norms(first, *results):
                def square(n):
                    c = n % NC
                    act.wait_ge(ln_xc_ready, n + 1)
                    if n >= 2:
                        act.wait_ge(ln_var_ready, n - 1)
                    f(ln_sq[:, c % 2, :], chunk(ln_xc, c), ACT.Square).then_inc(ln_sq_ready, 1)

                def std(n):
                    c = n % NC
                    if n == 0:
                        act.wait_ge(constants_ready, 1)
                    act.wait_ge(ln_var_ready, n + 1)
                    if n >= 2:
                        act.wait_ge(ln_rstd_ready, n - 1)
                    f(ln_std[:, c % 2, :], psum[:, 4 + c, 0:TPC], ACT.Sqrt, bias=eps_col[:]).then_inc(ln_std_ready, 1)

                def scaled(n):
                    c = n % NC
                    dst, scale, bias, ready = results[n // NC - first]
                    if n == 0:
                        act.wait_ge(mod_ready, 2)
                    act.wait_ge(ln_xn_ready, n + 1)
                    f(chunk(dst, c), ln_xn[:, c % 2, :], ACT.Identity, scale=scale, bias=bias).then_inc(ready, 1)

                ln_steps(first, len(results), (square, 1), (std, 2), (scaled, 3))

            def ssm_inputs():
                for c in range(NC):
                    act.wait_ge(x1_ps, c + 1)
                    f(x1pad[:, 1 + c * C:1 + (c + 1) * C], psum[:, c, :], ACT.Identity,
                      bias=col("w1_b")).then_inc(x1_ready, 1)
                    act.wait_ge(v_ps, c + 1)
                    f(chunk(vT, c), psum[:, 4 + c, :], ACT.Silu, bias=col("v1_b")).then_inc(v_ready, 1)
                for c in range(NC):
                    act.wait_ge(conv_ready, c + 1)
                    f(chunk(uT, c), chunk(conv_y, c), ACT.Silu).then_inc(u_ready, 1)
                for hf in range(2):
                    act.wait_ge(dt_ps, 2 * hf + 2)
                    f(half(dt_abs, hf), banks(2 * hf, 2), ACT.Abs, bias=col("b_dt")).then_inc(dt_abs_ready, 1)
                    act.wait_ge(bc_ps, 2 * hf + 2)
                    f(half(bc_p1, hf), banks(4 + 2 * hf, 2), ACT.Identity).then_inc(bc_p1_ready, 1)
                f(expA[:], cols[:, A_LOG:A_LOG + NS], ACT.Exp).then_inc(expA_ready, 1)
                for hf in range(2):
                    act.wait_ge(dt_abs_ready, hf + 1)
                    f(half(dt_z, hf), half(dt_abs, hf), ACT.Exp, scale=-1.0).then_inc(dt_z_ready, 1)
                for hf in range(2):
                    act.wait_ge(dt_w_ready, hf + 1)
                    f(half(dt_ln, hf), half(dt_w, hf), ACT.Ln).then_inc(dt_ln_ready, 1)
                    f(half(dt_x, hf), banks(2 * hf, 2), ACT.Relu, bias=col("b_dt")).then_inc(dt_x_ready, 1)

            def ssm_scan():
                act.wait_ge(negA_ready, 1)
                for hf in range(2):
                    act.wait_ge(dt_ready, hf + 1)
                    with act.Fori(0, NS // UNS) as i:
                        for k in range(UNS):
                            n = i * UNS + (hf * NS + k)
                            act.wait_ge(b_bc_ready, n + 1)
                            act.wait_ge(dBu_ready, n + 1)
                            f(ssm_b[:, k % 2, :], banks(0, 2), ACT.Identity).then_inc(b_copied, 1)
                            act.wait_ge(scan_done, n + 1)
                            f(ssm_dA[:, k % 2, :], half(dtT, hf), ACT.Exp,
                              scale=negA[:, bass.ds(i * UNS + k, 1)]).then_inc(dA_ready, 1)

            def ssm_out():
                act.wait_ge(mod_ready, 2)
                for c in range(NC):
                    act.wait_ge(w2_ps, c + 1)
                    if c >= 2:
                        act.wait_ge(ln_in_ready, NC + c - 1)
                    f(proj_o[:, c % 2, :], psum[:, c, :], ACT.Identity, bias=gated_w2b[:],
                      scale=modc(0, GA)).then_inc(w2_o_ready, 1)

            def route(layer):
                m = ms[layer]
                act.wait_ge(m["route_step"], 3)
                f(rt["prob"][:], rt["logit"][:], ACT.Exp).then_inc(m["exp_ready"], 1)

            def experts(layer):
                m = ms[layer]
                act.sem_inc(m["hid_ready"], HC)

                def hid(i, k, tb):
                    n = i * 2 * NC + (k * NC + tb)
                    act.wait_ge(m["out_ps"], n + 1)
                    for hc in range(HC):
                        act.wait_ge(m["hid_ps"], n * HC + (hc + 1))
                        if layer == 0:
                            f(hidden[:, tb % 2, hc, :], psum[:, hc, :], ACT.Silu, bias=b1s[:, k, hc:hc + 1]).then_inc(m["hid_ready"], 1)
                        else:
                            f(hidden[:, tb % 2, hc, :], psum[:, hc, :], ACT.Gelu).then_inc(m["hid_ready"], 1)

                def keep(n):
                    k, tb = n // NC, n % NC
                    act.wait_ge(m["out_ps"], n + 3)
                    f(chunk(early_out[:, k, :], tb), psum[:, 4 + tb % 2, :], ACT.Identity, bias=b2s[:, k, :]).then_inc(early_copied, 1)

                for n in range(2 * NC):
                    hid(0, n // NC, n % NC)
                    if n == 1:
                        act.wait_ge(m["rep_ps"], 1)
                        f(gates_rep[:], banks(4, 4), ACT.Identity).then_inc(m["rep_ready"], 1)
                    elif n and layer == 0:
                        keep(n - 2)
                if layer == 0:
                    for n in range(EARLY * NC - 2, EARLY * NC):
                        keep(n)
                with act.Fori(1, NE // 2) as i:
                    for k in range(2):
                        for tb in range(NC):
                            hid(i, k, tb)

            def attention_inputs():
                def raw(m):
                    c, j = m // 2, m % 2
                    act.wait_ge(qk_ps, m + 1)
                    f(chunk(qkT[j], c), psum[:, 4 + j, :], ACT.Identity, bias=col(("bq", "bk")[j])).then_inc(qk_raw, 1)

                def hi(m):
                    c, j = m // 2, m % 2
                    act.wait_ge(roped, m + 1)
                    f(chunk(qk_parts[j][:, 0, :], c), chunk(qkT[j], c), ACT.Identity).then_inc(hi_ready, 1)

                def mid(m):
                    c, j = m // 2, m % 2
                    act.wait_ge(rest_ready, m + 1)
                    f(chunk(qk_parts[j][:, 1, :], c), qk_rest[:, m % 2, :], ACT.Identity).then_inc(mid_ready, 1)

                raw(0)
                raw(1)
                for m in range(2 * NC + 1):
                    if m + 2 < 2 * NC:
                        raw(m + 2)
                    if m < 2 * NC:
                        hi(m)
                    if m:
                        mid(m - 1)

            def attention():
                act.sem_inc(p_ready, 2)
                act.sem_inc(o_copied, 1)
                for k in range(2):
                    act.sem_inc(o_stored[k], 16 * STORES)

                def row(hs, u, p):
                    act.wait_ge(s1_ps, hs * SN + (p + 1))
                    x = STREAM[p][2]
                    f(q_stack[0:SHIFT, u, x * C:(x + 1) * C], psum[0:SHIFT, 4 + p % RING, :], ACT.Identity).then_inc(row_copied, 1)

                def head(h, u, turn, following=True):
                    for t in range(2 * KT):
                        kt, b = t // 2, t % 2
                        act.wait_ge(s2_ps, h * 2 * KT + (t + 1))
                        if b == 0:
                            act.wait_ge(pv_done, h * KT + (kt + 1))
                        f(probs[:, kt % 4, b * HALF:(b + 1) * HALF], banks(2 * b, 2), ACT.Exp, scale=SCALE).then_inc(p_ready, 1)
                        for p in range(SN):
                            at = 2 * (STREAM[p][0] - AHEAD) + (1 if STREAM[p][0] == KT else 2)
                            if following and STREAM[p][1] == "row" and t == at:
                                row(h + 1, (u + 1) % UN, p)
                    act.wait_ge(pv_done, h * KT + (KT + 4))
                    act.wait_ge(o_stored[u % 2], turn * (16 * STORES * UN // 2) + 16 * STORES * (u // 2 + 1))
                    f(o_sb[:, u % 2, :], psum[:, 7, :], ACT.Identity).then_inc(o_copied, 1)

                act.sem_inc(row_copied, ROWS)
                for p in range(SN):
                    if STREAM[p][1] == "row":
                        row(0, 0, p)
                with act.Fori(0, NH // UN - 1) as i:
                    for u in range(UN):
                        head(i * UN + u, u, i)
                for u in range(UN):
                    head(NH - UN + u, u, NH // UN - 1, following=u < UN - 1)

            def attention_out():
                for c in range(NC):
                    act.wait_ge(wo_ps, c + 1)
                    if c >= 2:
                        act.wait_ge(ln_in_ready, 3 * NC + c - 1)
                    f(proj_o[:, c % 2, :], psum[:, 4 + c, :], ACT.Identity, bias=gated_bo[:],
                      scale=modc(1, GA)).then_inc(wo_o_ready, 1)

            modulation()
            layer_norms(0, (h0T, modc(0, CA), modc(0, SA), ln_in_ready), (normT, col("ln_g"), col("ln_b"), normed_ready))
            ssm_inputs()
            ssm_scan()
            ssm_out()
            layer_norms(2, (normT, modc(0, CB), modc(0, SB), normed_ready))
            route(0)
            experts(0)
            layer_norms(3, (normT, modc(1, CA), modc(1, SA), normed_ready))
            attention_inputs()
            attention()
            attention_out()
            layer_norms(4, (normT, modc(1, CB), modc(1, SB), normed_ready))
            route(1)
            experts(1)

        @block.gpsimd
        def _(pool):
            g = nc.gpsimd

            def ssm_inputs():
                for hf in range(2):
                    pool.wait_ge(bc_r1_ready, hf + 1)
                    g.tensor_copy(half(bc_p2, hf), half(bc_r1, hf)).then_inc(bc_p2_ready, 1)

            def ssm_scan():
                for hf in range(2):
                    pool.wait_ge(dtu_ready, hf + 1)
                    with pool.Fori(0, NS // UNS) as i:
                        for k in range(UNS):
                            n = i * UNS + (hf * NS + k)
                            pool.wait_ge(b_copied, n + 1)
                            pool.wait_ge(scan_done, n + 1)
                            g.tensor_tensor(ssm_dBu[:, k % 2, :], half(dtuT, hf), ssm_b[:, k % 2, :], ALU.mult).then_inc(dBu_ready, 1)

            def experts(layer):
                m = ms[layer]
                def add(n, tb, gated_sem, value):
                    pool.wait_ge(gated_sem, value)
                    pool.wait_ge(m["acc_done"], n + 2)
                    g.tensor_tensor(chunk(moe_acc, tb), chunk(moe_acc, tb), gated[:, tb % 2, :],
                                    ALU.add).then_inc(m["acc_done"], 1)

                if layer == 0:
                    pool.sem_inc(m["acc_done"], 2 + NC)
                    for n in range(NC, EARLY * NC):
                        add(n, n % NC, early_gated, n + 1)
                else:
                    pool.sem_inc(m["acc_done"], 1)
                    pool.wait_ge(ln_in_ready, 2 * NC * (layer + 1))
                    g.memset(moe_acc[:], 0.0).then_inc(m["acc_done"], 1)
                with pool.Fori(0 if layer else 1, NE // 2) as i:
                    for k in range(2):
                        for tb in range(NC):
                            n = i * 2 * NC + (k * NC + tb)
                            add(n, tb, m["out_gated"], n + 3)

            def attention_inputs():
                pool.wait_ge(ln_in_ready, 3 * NC)
                pool.wait_ge(tables_in, 48)
                for m in range(2 * NC):
                    c, j = m // 2, m % 2
                    pool.wait_ge(qk_raw, m + 1)
                    if m >= 2:
                        pool.wait_ge(roped, m - 1)
                    g.tensor_tensor(rope_cos[:, m % 2, :], chunk(qkT[j], c), chunk(cosT, c), ALU.mult).then_inc(cos_ready, 1)
                for t in (q_stack, k_stack):
                    g.memset(t[:].bitcast(F32), 0.0).then_inc(stack_step, 1)
                pool.wait_ge(stack_step, 2)
                g.memset(k_stack[0:SHIFT].bitcast(F32), TWO_MINUS_ONES).then_inc(stacks_clear, 1)
                g.memset(v_head[:], 0.0).then_inc(v_pad, 1)
                g.memset(v_all[:, :, :, HD:HD + 1], 1.0).then_inc(v_pad, 1)

            def attention():
                pool.wait_ge(v_pad, 2)
                pool.wait_ge(v_all_ready, TILES)

                def head(h, u):
                    g.tensor_copy(v_head[:, u, :, 0:HD + 1], v_all[:, :, bass.ds(h, 1), :].rearrange("p k o d -> p k (o d)")).then_inc(v_head_ready, 1)

                for u in range(UN):
                    head(u, u)
                with pool.Fori(1, NH // UN) as i:
                    for u in range(UN):
                        pool.wait_ge(pv_done, i * (UN * KT) + (KT * (u - UN + 1) + 4))
                        head(i * UN + u, u)

            ssm_inputs()
            ssm_scan()
            experts(0)
            attention_inputs()
            attention()
            experts(1)

        @block.vector
        def _(dve):
            v = nc.vector

            def constants():
                v.memset(eps_col[:], EPS).then_inc(constants_ready, 1)
                v.memset(x1pad[:, 0:1], 0.0).then_inc(pad_ready, 1)
                v.memset(x1pad[:, L + 1:L + 2], 0.0).then_inc(pad_ready, 1)
                dve.wait_ge(params_in, 48)
                v.tensor_copy(ident_b[:], mat("ident")).then_inc(constants_ready, 1)
                v.tensor_copy(bcsel[:], bcsel_f[:]).then_inc(bcsel_ready, 1)
                v.tensor_scalar(diag_skip[:], mat("ident"), col("D_skip"), None, ALU.mult).then_inc(diag_ready, 1)

            def modulation():
                dve.wait_ge(mod_ps_ready, 1)
                v.tensor_copy(mod[:], psum[:, 7, 0:12]).then_inc(mod_step, 1)
                dve.wait_ge(mod_step, 1)
                gates = mod[:].rearrange("p (a b) -> p a b", b=3)[:, :, GA:GA + 1]
                scales = mod[:].rearrange("p (a b) -> p a b", b=3)[:, :, CA:CA + 1]
                size, sign = (t[:].rearrange("p (a b) -> p a b", b=1) for t in (gate_size, gate_sign))
                v.tensor_scalar(scales, scales, 1.0, None, ALU.add).then_inc(mod_step, 1)
                v.tensor_scalar(sign, gates, 0.0, 2.0, ALU.is_ge, ALU.mult).then_inc(mod_step, 1)
                dve.wait_ge(mod_step, 3)
                v.tensor_scalar(sign, sign, -1.0, None, ALU.add).then_inc(mod_step, 1)
                dve.wait_ge(mod_step, 4)
                v.tensor_tensor(size, gates, sign, ALU.mult).then_inc(mod_step, 1)
                dve.wait_ge(mod_step, 5)
                v.scalar_tensor_tensor(gates, size, 0.25, sign, ALU.max, ALU.mult).then_inc(mod_step, 1)
                dve.wait_ge(mod_step, 6)
                v.tensor_tensor(gated_bo[:], col("bo"), modc(1, GA), ALU.mult).then_inc(mod_ready, 1)
                v.tensor_tensor(gated_w2b[:], col("w2_b"), modc(0, GA), ALU.mult).then_inc(mod_ready, 1)

            def layer_norms(first, *sources):
                def centre(n):
                    c = n % NC
                    dve.wait_ge(ln_mean_ready, n + 1)
                    if n // NC > first:
                        dve.wait_ge(ln_xn_ready, n - NC + 1)
                    v.tensor_tensor(chunk(ln_xc, c), chunk(sources[n // NC - first], c), psum[:, c, :], ALU.subtract).then_inc(ln_xc_ready, 1)
                    if n == 1:
                        modulation()

                def rstd(n):
                    c = n % NC
                    dve.wait_ge(ln_std_ready, n + 1)
                    if n >= 2:
                        dve.wait_ge(ln_bc_ready, n - 1)
                    v.reciprocal(ln_rstd[:, c % 2, :], ln_std[:, c % 2, :]).then_inc(ln_rstd_ready, 1)

                def normed(n):
                    c = n % NC
                    dve.wait_ge(ln_bc_ready, n + 1)
                    if n // NC <= 1 and 2 <= n < NC + 2:
                        dve.wait_ge(ln_in_ready, n - 1)
                    elif n >= 2:
                        dve.wait_ge(normed_ready, n - 1 - NC)
                    v.tensor_tensor(ln_xn[:, c % 2, :], chunk(ln_xc, c), psum[:, 4 + c, :], ALU.mult).then_inc(ln_xn_ready, 1)

                ln_steps(first, len(sources), (normed, 3), (centre, 0), (rstd, 2))

            def ssm_inputs():
                dve.wait_ge(pad_ready, 2)
                for c in range(NC):
                    s, at = c % 2, c * C
                    dve.wait_ge(x1_ready, min(c + 2, NC))
                    v.tensor_scalar(conv_a[:, s, :], x1pad[:, at:at + C], col("conv0"), None, ALU.mult).then_inc(conv_step, 1)
                    dve.wait_ge(conv_step, 2 * c + 1)
                    v.scalar_tensor_tensor(conv_b[:, s, :], x1pad[:, at + 1:at + 1 + C], col("conv1"), conv_a[:, s, :],
                                           ALU.mult, ALU.add).then_inc(conv_step, 1)
                    dve.wait_ge(conv_step, 2 * c + 2)
                    v.scalar_tensor_tensor(chunk(conv_y, c), x1pad[:, at + 2:at + 2 + C], col("conv2"), conv_b[:, s, :],
                                           ALU.mult, ALU.add).then_inc(conv_ready, 1)
                for hf in range(2):
                    dve.wait_ge(bc_p1_ready, hf + 1)
                    v.scalar_tensor_tensor(half(bc_r1, hf), half(bc_p1, hf), col("part1"), banks(4 + 2 * hf, 2),
                                           ALU.mult, ALU.add).then_inc(bc_r1_ready, 1)
                dve.wait_ge(expA_ready, 1)
                v.tensor_scalar(negA[:], expA[:], -1.0, None, ALU.mult).then_inc(negA_ready, 1)
                for hf in range(2):
                    dve.wait_ge(dt_z_ready, hf + 1)
                    v.tensor_scalar(half(dt_w, hf), half(dt_z, hf), 1.0, None, ALU.add).then_inc(dt_w_ready, 1)
                for hf in range(2):
                    dve.wait_ge(dt_w_ready, hf + 1)
                    v.scalar_tensor_tensor(half(dt_e, hf), half(dt_w, hf), 1.0, half(dt_z, hf),
                                           ALU.subtract, ALU.subtract).then_inc(dt_e_ready, 1)
                for hf in range(2):
                    dve.wait_ge(bc_p2_ready, hf + 1)
                    dve.wait_ge(bc_r1_ready, hf + 1)
                    v.scalar_tensor_tensor(half(bc_parts, hf), half(bc_p2, hf), col("part2"), half(bc_r1, hf),
                                           ALU.mult, ALU.add).then_inc(bc_parts_ready, 1)
                    dve.wait_ge(dt_e_ready, hf + 1)
                    dve.wait_ge(dt_ln_ready, hf + 1)
                    v.tensor_tensor(half(dt_r, hf), half(dt_ln, hf), half(dt_e, hf), ALU.subtract).then_inc(dt_r_ready, 1)
                    dve.wait_ge(dt_r_ready, hf + 1)
                    dve.wait_ge(dt_x_ready, hf + 1)
                    v.tensor_tensor(half(dtT, hf), half(dt_x, hf), half(dt_r, hf), ALU.add).then_inc(dt_ready, 1)
                    dve.wait_ge(dt_ready, hf + 1)
                    v.tensor_tensor(half(dtuT, hf), half(dtT, hf), half(uT, hf), ALU.mult).then_inc(dtu_ready, 1)

            def ssm_scan():
                dve.wait_ge(dtu_ready, 2)
                dve.sem_inc(dBu_ready, 2)
                dve.sem_inc(g_ready, 2)
                dve.sem_inc(scan_done, 2)
                dve.sem_inc(carry_done, 2)
                for hf in range(2):
                    with dve.Fori(0, NS // UNS) as i:
                        for k in range(UNS):
                            n = i * UNS + (hf * NS + k)
                            at = bass.ds(i * UNS + k, 1)
                            s = k % 2
                            dve.wait_ge(dBu_ready, n + 3)
                            dve.wait_ge(dA_ready, n + 1)
                            dve.wait_ge(g_ready, n + 1)
                            dve.wait_ge(carry_done, n + 1)
                            v.tensor_tensor_scan(ssm_h[:, s, :], ssm_dA[:, s, :], ssm_dBu[:, s, :],
                                                 ssm_carry[:, at] if hf else 0.0,
                                                 ALU.mult, ALU.add).then_inc(scan_done, 1)
                            dve.wait_ge(c_bc_ready, n + 1)
                            dve.wait_ge(scan_done, n + 3)
                            dve.wait_ge(y_added, n + 1)
                            v.tensor_tensor(ssm_g[:, s, :], ssm_h[:, s, :], banks(c_bank(hf, s), 2), ALU.mult).then_inc(g_ready, 1)
                            v.tensor_copy(ssm_carry[:, at], ssm_h[:, s, HALF - 1:HALF]).then_inc(carry_done, 1)
                    dve.wait_ge(y_added, 2 + NS * (hf + 1))
                    v.tensor_tensor(half(yvT, hf), banks(4 + 2 * hf, 2), half(vT, hf), ALU.mult).then_inc(yv_ready, 1)

            def residual(ready):
                for c in range(NC):
                    dve.wait_ge(ready, c + 1)
                    v.tensor_tensor(chunk(xT, c), chunk(xT, c), proj_o[:, c % 2, :], ALU.add).then_inc(ln_in_ready, 1)

            def route(layer):
                m = ms[layer]
                steps = [0]

                def step(i):
                    steps[0] += 1
                    i.then_inc(m["route_step"], 1)
                    dve.wait_ge(m["route_step"], steps[0])

                def wide(t):
                    return t[:].unsqueeze(2).to_broadcast([128, TILES, NE])

                def each(t):
                    return t.unsqueeze(1).to_broadcast([128, TILES, NE])

                logits = psum[:, 4, 0:TILES * NE].rearrange("p (t e) -> p t e", e=NE)
                dve.wait_ge(m["logits_ready"], 1)
                if layer == 0:
                    step(v.tensor_tensor(rt["logit"][:], logits, each(router_b), ALU.add))
                else:
                    step(v.tensor_copy(rt["logit"][:], logits))
                step(v.tensor_reduce(rs["max"][:], rt["logit"][:], AX.X, ALU.max))
                step(v.tensor_tensor(rt["logit"][:], rt["logit"][:], wide(rs["max"]), ALU.subtract))
                dve.wait_ge(m["exp_ready"], 1)
                step(v.tensor_reduce(rs["sum"][:], rt["prob"][:], AX.X, ALU.add))
                step(v.reciprocal(rs["inv"][:], rs["sum"][:]))
                step(v.tensor_tensor(rt["prob"][:], rt["prob"][:], wide(rs["inv"]), ALU.mult))

                def best(src, top, out):
                    step(v.tensor_reduce(rs[top][:], rt[src][:], AX.X, ALU.max))
                    step(v.tensor_tensor(rt["eq"][:], rt[src][:], wide(rs[top]), ALU.is_equal))
                    step(v.tensor_tensor(rt["eq"][:], rt["eq"][:], each(expert_no), ALU.mult))
                    step(v.tensor_reduce(rs["no"][:], rt["eq"][:], AX.X, ALU.min))
                    step(v.tensor_tensor(rt[out][:], wide(rs["no"]), each(expert_no), ALU.is_equal))

                best("prob", "top1", "best1")
                step(v.scalar_tensor_tensor(rt["rest"][:], rt["best1"][:], -4.0, rt["prob"][:], ALU.mult, ALU.add))
                best("rest", "top2", "best2")
                step(v.tensor_tensor(rt["best1"][:], rt["best1"][:], rt["best2"][:], ALU.add))
                step(v.tensor_tensor(rt["gate"][:], rt["best1"][:], rt["prob"][:], ALU.mult))
                if layer == 1:
                    step(v.tensor_tensor(rs["sum"][:], rs["top1"][:], rs["top2"][:], ALU.add))
                    step(v.reciprocal(rs["inv"][:], rs["sum"][:]))
                    step(v.tensor_tensor(rt["gate"][:], rt["gate"][:], wide(rs["inv"]), ALU.mult))
                v.tensor_copy(gate_wide, rt["gate"][:].unsqueeze(3).to_broadcast([128, TILES, NE, REP])).then_inc(m["wide_ready"], 1)

            def keep_capacity():
                m = ms[0]
                dve.wait_ge(m["rep_ready"], 1)
                v.memset(thr["low"][:], 0).then_inc(m["thr_step"], 1)
                with dve.Fori(0, ROUNDS) as r:
                    at = bass.ds(r, 1)
                    dve.wait_ge(m["thr_step"], r * 6 + 1)
                    v.tensor_tensor(thr["try"][:], thr["low"][:], digits[:, at], ALU.bitwise_or).then_inc(m["thr_step"], 1)
                    dve.wait_ge(m["thr_step"], r * 6 + 2)
                    v.tensor_scalar(gate_eq[:], gates_rep[:], thr["try"][:].bitcast(F32), None, ALU.is_ge,
                                    ALU.add, accum_out=thr_f["count"][:]).then_inc(thr_count_done, 1)
                    dve.wait_ge(thr_count_done, r + 1)
                    v.tensor_scalar(thr_f["keep"][:], thr_f["count"][:], CAP - 0.5, None, ALU.is_ge).then_inc(m["thr_step"], 1)
                    dve.wait_ge(m["thr_counted"], r + 1)
                    v.tensor_scalar(thr["add"][:], psum[:, 6, 0:1], -1.0, digit_size[:, at], ALU.add, ALU.mult).then_inc(m["thr_step"], 1)
                    dve.wait_ge(m["thr_step"], r * 6 + 4)
                    v.tensor_tensor(thr["low"][:], thr["low"][:], thr["add"][:], ALU.bitwise_or).then_inc(m["thr_step"], 3)
                low = thr["low"][:].bitcast(F32)
                base = [ROUNDS * 6 + 1]

                def step(i):
                    base[0] += 1
                    i.then_inc(m["thr_step"], 1)
                    dve.wait_ge(m["thr_step"], base[0])

                dve.wait_ge(m["thr_step"], base[0])
                step(v.tensor_scalar(gate_eq[:], gates_rep[:], low, None, ALU.is_gt, ALU.add, accum_out=thr_f["count"][:]))
                step(v.tensor_scalar(thr_f["quota"][:], thr_f["count"][:], -1.0, float(CAP), ALU.mult, ALU.add))
                step(v.tensor_scalar(gate_eq[:], gates_rep[:], low, None, ALU.is_equal))
                step(v.tensor_tensor_scan(gate_rank[:], gate_eq[:], gate_eq[:], 0.0, ALU.add, ALU.max))
                step(v.scalar_tensor_tensor(gate_eq[:], gate_rank[:], thr_f["quota"][:], gate_eq[:], ALU.is_le, ALU.mult))
                step(v.scalar_tensor_tensor(gate_eq[:], gates_rep[:], low, gate_eq[:], ALU.is_gt, ALU.add))
                v.tensor_tensor(gate_valid[:], gates_rep[:], gate_eq[:], ALU.mult).then_inc(m["gates_final"], 1)

            def experts(layer):
                m = ms[layer]
                dve.sem_inc(m["out_gated"], 2 if layer else 2 + EARLY * NC)
                if layer == 0:
                    for n in range(EARLY * NC):
                        k, tb = n // NC, n % NC
                        if tb == 0:
                            dve.wait_ge(m["gates_in"][k], 16)
                        dve.wait_ge(early_copied, n + 1)
                        o, g = chunk(early_out[:, k, :], tb), gate_bc[:, k, tb * C:(tb + 1) * C]
                        if k == 0:
                            v.tensor_tensor(chunk(moe_acc, tb), o, g, ALU.mult).then_inc(early_gated, 1)
                        else:
                            dve.wait_ge(m["acc_done"], n + 1)
                            v.tensor_tensor(gated[:, tb % 2, :], o, g, ALU.mult).then_inc(early_gated, 1)
                with dve.Fori(0 if layer else 1, NE // 2) as i:
                    for k in range(2):
                        dve.wait_ge(m["gates_in"][k], (i + 1) * 16)
                        for tb in range(NC):
                            n = i * 2 * NC + (k * NC + tb)
                            dve.wait_ge(m["out_ps"], n + 3)
                            dve.wait_ge(m["acc_done"], n + 1)
                            o, a, g = gated[:, tb % 2, :], psum[:, 4 + tb % 2, :], gate_bc[:, k, tb * C:(tb + 1) * C]
                            if layer == 0:
                                j = v.scalar_tensor_tensor(o, a, b2s[:, k, :], g, ALU.add, ALU.mult)
                            else:
                                j = v.tensor_tensor(o, a, g, ALU.mult)
                            j.then_inc(m["out_gated"], 1)
                for c in range(NC):
                    dve.wait_ge(m["acc_done"], 2 + NE * NC - (NC - 1 - c))
                    v.scalar_tensor_tensor(chunk(xT, c), chunk(moe_acc, c), modc(layer, GB), chunk(xT, c),
                                           ALU.mult, ALU.add).then_inc(ln_in_ready, 1)

            def attention_inputs():
                dve.wait_ge(tables_in, 48)

                def rope(m):
                    c, j = m // 2, m % 2
                    dve.wait_ge(rot_ps, m + 1)
                    v.tensor_tensor(rope_sin[:, m % 2, :], psum[:, 6 + j, :], chunk(sinT, c), ALU.mult).then_inc(sin_ready, 1)
                    dve.wait_ge(sin_ready, m + 1)
                    dve.wait_ge(cos_ready, m + 1)
                    v.tensor_tensor(chunk(qkT[j], c), rope_cos[:, m % 2, :], rope_sin[:, m % 2, :], ALU.add).then_inc(roped, 1)

                def rest(m):
                    c, j = m // 2, m % 2
                    if m >= 2:
                        dve.wait_ge(lo_ready, m - 1)
                    dve.wait_ge(hi_ready, m + 1)
                    dve.wait_ge(roped, m + 1)
                    v.tensor_tensor(qk_rest[:, m % 2, :], chunk(qkT[j], c), chunk(qk_parts[j][:, 0, :], c), ALU.subtract).then_inc(rest_ready, 1)

                def low(m):
                    c, j = m // 2, m % 2
                    dve.wait_ge(mid_ready, m + 1)
                    dve.wait_ge(rest_ready, m + 1)
                    v.tensor_tensor(chunk(qk_parts[j][:, 2, :], c), qk_rest[:, m % 2, :], chunk(qk_parts[j][:, 1, :], c), ALU.subtract).then_inc(lo_ready, 1)

                for m in range(2 * NC + 2):
                    if m < 2 * NC:
                        rope(m)
                    if 0 <= m - 1 < 2 * NC:
                        rest(m - 1)
                    if 0 <= m - 2:
                        low(m - 2)
                dve.wait_ge(v_pad, 2)
                dve.wait_ge(mats_loaded, 16)
                bv = mat("bv_rows").rearrange("p (h d) -> p h d", h=NH)
                for t in range(TILES):
                    dve.wait_ge(av_ps, TPC * (t // TPC) + TPC)
                    src = psum[:, t // TPC, (t % TPC) * 128:(t % TPC + 1) * 128].rearrange("p (h d) -> p h d", h=NH)
                    v.tensor_tensor(v_all[:, t, :, 0:HD], src, bv, ALU.add).then_inc(v_all_ready, 1)

            def attention():
                dve.sem_inc(s1_read, RING)

                def head(hs, u):
                    for p in range(SN):
                        step, kind, x = STREAM[p]
                        if kind == "row":
                            continue
                        qt, c = x
                        dve.wait_ge(s1_ps, hs * SN + (p + 1))
                        v.tensor_reduce(tile_max[:, qt, c:c + 1], psum[:, 4 + p % RING, :], AX.X, ALU.max).then_inc(s1_read, 1)
                        if qt % 4 == 3 and c == NC - 1:
                            g = qt // 4
                            dve.wait_ge(s1_read, hs * SCORES + ((qt + 1) * NC + RING))
                            v.tensor_reduce(row_max[:, g, :], tile_max[:, 4 * g:4 * g + 4, :], AX.X, ALU.max).then_inc(max_step, 1)
                            dve.wait_ge(max_step, hs * 8 + (2 * g + 1))
                            v.tensor_copy(max_parts[:, g, :, 0], row_max[:, g, :]).then_inc(max_step, 1)
                            dve.wait_ge(max_step, hs * 8 + (2 * g + 2))
                            v.tensor_tensor(max_parts[:, g, :, 1], row_max[:, g, :], max_parts[:, g, :, 0], ALU.subtract).then_inc(max_parts_ready, 1)

                with dve.Fori(0, NH // UN) as i:
                    for u in range(UN):
                        head(i * UN + u, u)
                dve.wait_ge(o_in, 32)
                for k in range(2):
                    dve.wait_ge(o_stored[k], 16 * STORES * (1 + NH // 2))
                v.reciprocal(sums[:], sums[:]).then_inc(inv_ready, 1)
                for c in range(NC):
                    dve.wait_ge(inv_ps, c + 1)
                    v.tensor_tensor(chunk(attnT, c), chunk(attnT, c), psum[:, c, :], ALU.mult).then_inc(attn_ready, 1)

            constants()
            dve.sem_inc(y_added, 2)
            layer_norms(0, xT, h0T)
            ssm_inputs()
            ssm_scan()
            residual(w2_o_ready)
            layer_norms(2, xT)
            route(0)
            keep_capacity()
            experts(0)
            layer_norms(3, xT)
            attention_inputs()
            attention()
            residual(wo_o_ready)
            layer_norms(4, xT)
            route(1)
            experts(1)


def kernel(**inputs):
    import concourse.bacc as bacc
    from concourse.bass_utils import run_bass_kernel_spmd

    g = {k: np.ascontiguousarray(a) for k, a in inputs.items()}
    ident = np.eye(128, dtype=np.float32)
    quadrant = np.arange(128) // 32
    rotate = np.zeros((128, 128), np.float32)
    rotate[np.arange(1, 128, 2), np.arange(0, 128, 2)] = -1.0
    rotate[np.arange(0, 128, 2), np.arange(1, 128, 2)] = 1.0
    inv_freq = (1.0 / np.float32(THETA) ** (np.arange(0, HD, 2, dtype=np.float32) / np.float32(HD))).astype(np.float32)
    angles = np.tile(np.repeat(np.arange(L, dtype=np.float32)[:, None] * inv_freq[None, :], 2, axis=1), (1, NH)).T
    vectors = {
        "ln_g": g["L0_attn_ln_g"], "ln_b": g["L0_attn_ln_b"], "w1_b": g["L0_attn_w1_b"], "v1_b": g["L0_attn_v1_b"],
        "w2_b": g["L0_attn_w2_b"], "b_dt": g["L0_attn_b_dt"], "D_skip": g["L0_attn_D_skip"],
        "conv0": g["L0_attn_conv_w"][:, 0, 0], "conv1": g["L0_attn_conv_w"][:, 0, 1], "conv2": g["L0_attn_conv_w"][:, 0, 2],
        "c0": g["L0_c"][0], "c1": g["L1_c"][0], "bq": g["L1_attn_bq"], "bk": g["L1_attn_bk"], "bo": g["L1_attn_bo"],
        "part1": np.where(quadrant >= 1, -1.0, 0.0).astype(np.float32),
        "part2": np.where(quadrant >= 2, -1.0, 0.0).astype(np.float32),
    }
    cols = np.concatenate([np.stack([vectors[n] for n in COLS], 1), g["L0_attn_A_log"]], 1)
    bc = np.concatenate([g["L0_attn_W_B"], g["L0_attn_W_C"]], 1)
    matrices = {
        "w1": g["L0_attn_w1_w"], "v1": g["L0_attn_v1_w"], "w2": g["L0_attn_w2_w"], "W_dt": g["L0_attn_W_dt"],
        "W_BC": np.concatenate([bc, bc, bc, np.zeros((128, 32), np.float32)], 1),
        "WqT": g["L1_attn_Wq"].T, "WkT": g["L1_attn_Wk"].T, "WvT": g["L1_attn_Wv"].T, "WoT": g["L1_attn_Wo"].T,
        "ident": ident, "mean": np.full((128, 128), 1.0 / D, np.float32),
        "bv_rows": np.broadcast_to(g["L1_attn_bv"], (128, 128)), "rotate": rotate,
        "group": (np.arange(128)[:, None] // REP == np.arange(128)[None, :] // REP).astype(np.float32),
    }
    mats = np.stack([matrices[n] for n in MATS], 1)
    wmod = np.concatenate([g["L0_wmod"].reshape(128, 6, 128), g["L1_wmod"].reshape(128, 6, 128)], 1)
    p = np.arange(128)[:, None]
    bcsel = ((p % 32 == np.arange(32)[None, :]) & (p < 96)).astype(np.float32)
    spread = ((p[:, :, None] % HD == np.arange(HD)[None, :, None]) & (p[:, :, None] // HD == np.arange(128) // HD)).astype(np.float32)
    shifts = 4 * np.arange(ROUNDS - 1, -1, -1)
    digit = np.minimum(p % REP, np.where(shifts == 28, 4, REP)) << shifts
    router = np.concatenate([
        g["L0_ffn_Wr"], g["L1_ffn_router_w"].T, np.broadcast_to(np.arange(NE, dtype=np.float32) - NE, (128, NE)),
        np.broadcast_to(g["L0_ffn_br"], (128, NE)), np.broadcast_to((2.0 ** shifts).astype(np.float32), (128, ROUNDS))], 1)
    arrays = {"xT_in": g["L0_attn_x"][0].T, "cols_in": cols, "mats_in": mats, "wmod_in": wmod, "bcsel_in": bcsel,
              "router_in": router, "digits_in": digit.astype(np.int32),
              "cos_in": np.cos(angles), "sin_in": np.sin(angles), "zero_in": np.zeros((SHIFT, L // 2), np.float32),
              "spread_in": spread}
    expert_arrays = [
        {"w1_0": g["L0_ffn_W1"], "w2_0": g["L0_ffn_W2"].reshape(NE, HC, 128, D).transpose(0, 2, 1, 3),
         "b1_0": g["L0_ffn_b1"].reshape(NE, HC, 128).transpose(0, 2, 1), "b2_0": g["L0_ffn_b2"][:, :, None]},
        {"w1_1": g["L1_ffn_w1"], "w2_1": g["L1_ffn_w2"].reshape(NE, HC, 128, D).transpose(0, 2, 1, 3)},
    ]
    arrays.update(expert_arrays[0])
    arrays.update(expert_arrays[1])
    arrays = {k: np.ascontiguousarray(a) for k, a in arrays.items()}

    nc = bacc.Bacc("TRN2", target_bir_lowering=False, num_devices=1)
    ins = {k: nc.dram_tensor(k, a.shape, mybir.dt.from_np(a.dtype), kind="ExternalInput").ap() for k, a in arrays.items()}
    moe_in = [[ins.pop(n) for n in e] for e in expert_arrays]
    out = nc.dram_tensor("outT", (128, L), F32, kind="ExternalOutput").ap()
    build(nc, *ins.values(), moe_in, out)
    r = run_bass_kernel_spmd(nc, [arrays], core_ids=[0])
    return np.ascontiguousarray(r.results[0]["outT"].T)[None]
```
